# Optimizing a Trainium2 kernel written in Bass

```python
import numpy as np
import jax
import jax.numpy as jnp

def _softmax(x, axis=-1):
    return jax.nn.softmax(x, axis=axis)

def _gelu(x):
    return jax.nn.gelu(x, approximate=True)

def _silu(x):
    return jax.nn.silu(x)

def _sigmoid(x):
    return jax.nn.sigmoid(x)

def _layernorm(x, axis=-1, eps=1e-05):
    m = jnp.mean(x, axis=axis, keepdims=True)
    v = jnp.var(x, axis=axis, keepdims=True)
    return (x - m) / jnp.sqrt(v + eps)

def _scatter_add(tgt, idx, src, axis=0):
    return tgt.at[idx].add(src)

def _segment_sum(src, seg, n):
    return jax.ops.segment_sum(src, seg, n)
kernel_name = 'mk_pixart_seq_d2_seqx_r4_1ea5ff'

def setup_inputs(seed: int=0):
    np.random.seed(seed)
    _w = jnp.asarray

    def _rec_inputs():
        import jax
        import jax.numpy as jnp
        _rk = jax.random.key(seed)
        x = 7.22e-05 + 1 * jax.random.normal(jax.random.fold_in(_rk, 1), (4, 512, 256), jnp.float32)
        _lenS = 512 - jax.random.randint(jax.random.fold_in(_rk, 7), (4,), 0, max(1, 512 // 4) + 1, jnp.int32)
        _lenS2 = 64 - jax.random.randint(jax.random.fold_in(_rk, 8), (4,), 0, max(1, 64 // 4) + 1, jnp.int32)
        cond_1024 = 0.0061147 + 1.02565 * jax.random.normal(jax.random.fold_in(_rk, 11), (4, 256), jnp.float32)
        _ctx_768P = jax.random.normal(jax.random.fold_in(_rk, 12), (4, 16, 192), jnp.float32)
        _ctx_768c = jax.random.dirichlet(jax.random.fold_in(_rk, 512), 0.3 * jnp.ones((16,), jnp.float32), (4, 64))
        _ctx_768t = jnp.einsum('bsk,bkd->bsd', _ctx_768c, _ctx_768P)
        _ctx_768t = _ctx_768t * jax.lax.rsqrt(jnp.mean(jnp.square(_ctx_768t)) + 1e-12) * 0.953939
        ctx_768 = 0.000599585 + 1.00006 * (_ctx_768t + 0.3 * jax.random.normal(jax.random.fold_in(_rk, 612), (4, 64, 192), jnp.float32))
        return (x, cond_1024, ctx_768)
    x, cond_1024, ctx_768 = _rec_inputs()

    def _L0_xcond_setup():
        import jax, jax.numpy as jnp
        import numpy as np
        EPS = 1e-05

        def _ada_ln(x, t, W, b):
            emb = t @ W + b
            scale, shift = jnp.split(emb, 2, axis=-1)
            mu = x.mean(-1, keepdims=True)
            var = ((x - mu) ** 2).mean(-1, keepdims=True)
            xn = (x - mu) * jax.lax.rsqrt(var + EPS)
            return xn * (1.0 + scale) + shift

        def _attn(x, ctx, Wq, Wk, Wv, Wo, bo, heads):
            b, n, _ = x.shape
            j = ctx.shape[1]
            q = (x @ Wq).reshape(b, n, heads, -1)
            k = (ctx @ Wk).reshape(b, j, heads, -1)
            v = (ctx @ Wv).reshape(b, j, heads, -1)
            scale = q.shape[-1] ** (-0.5)
            sim = jnp.einsum('bihd,bjhd->bhij', q, k) * scale
            attn = jax.nn.softmax(sim, axis=-1)
            out = jnp.einsum('bhij,bjhd->bihd', attn, v).reshape(b, n, -1)
            return out @ Wo + bo

        def _ff(x, W1, b1, W2, b2):
            p = x @ W1 + b1
            a, gate = jnp.split(p, 2, axis=-1)
            return a * jax.nn.gelu(gate, approximate=False) @ W2 + b2
        key = jax.random.key(seed)
        ks = jax.random.split(key, 32)
        B, N, D = (4, 512, 256)
        J, CD = (64, 192)
        H, DH = (16, 64)
        INNER = H * DH
        FF = 4 * D
        w = lambda k, shp: jax.random.normal(k, shp, jnp.float32) * 0.02
        inp = {'x': jax.random.normal(ks[0], (B, N, D), jnp.float32), 't': jax.random.normal(ks[1], (B, 1, D), jnp.float32), 'context': jax.random.normal(ks[2], (B, J, CD), jnp.float32), 'n1_w': w(ks[3], (D, 2 * D)), 'n1_b': jnp.zeros((2 * D,), jnp.float32), 'n2_w': w(ks[4], (D, 2 * D)), 'n2_b': jnp.zeros((2 * D,), jnp.float32), 'n3_w': w(ks[5], (D, 2 * D)), 'n3_b': jnp.zeros((2 * D,), jnp.float32), 'q1': w(ks[6], (D, INNER)), 'k1': w(ks[7], (D, INNER)), 'v1': w(ks[8], (D, INNER)), 'o1_w': w(ks[9], (INNER, D)), 'o1_b': jnp.zeros((D,), jnp.float32), 'q2': w(ks[10], (D, INNER)), 'k2': w(ks[11], (CD, INNER)), 'v2': w(ks[12], (CD, INNER)), 'o2_w': w(ks[13], (INNER, D)), 'o2_b': jnp.zeros((D,), jnp.float32), 'ff_w1': w(ks[14], (D, 2 * FF)), 'ff_b1': jnp.zeros((2 * FF,), jnp.float32), 'ff_w2': w(ks[15], (FF, D)), 'ff_b2': jnp.zeros((D,), jnp.float32)}
        return inp
    _L0_xcond_all = _L0_xcond_setup()
    _L0_xcond_in = {k: v for k, v in _L0_xcond_all.items() if k in ('n1_w', 'n1_b', 'n2_w', 'n2_b', 'n3_w', 'n3_b', 'q1', 'k1', 'v1', 'o1_w', 'o1_b', 'q2', 'k2', 'v2', 'o2_w', 'o2_b', 'ff_w1', 'ff_b1', 'ff_w2', 'ff_b2')}
    del _L0_xcond_all

    def _L1_xcond_setup():
        import jax, jax.numpy as jnp
        import numpy as np
        B, N, M = (2, 256, 128)
        D, H, DH = (256, 16, 64)
        MID = H * DH
        DC = 192
        MULT = 4
        EPS = 1e-05

        def _ln(x, w, b):
            mu = jnp.mean(x, -1, keepdims=True)
            var = jnp.mean((x - mu) ** 2, -1, keepdims=True)
            return (x - mu) * jax.lax.rsqrt(var + EPS) * w + b

        def _sincos(n, d):
            inv = 1.0 / 10000.0 ** (jnp.arange(0, d, 2, dtype=jnp.float32) / d)
            ang = jnp.arange(n, dtype=jnp.float32)[:, None] * inv[None, :]
            return (jnp.sin(ang), jnp.cos(ang))

        def _rope(x, sin, cos):
            s = sin[None, None]
            c = cos[None, None]
            xe = x[..., ::2]
            xo = x[..., 1::2]
            re = xe * c - xo * s
            ro = xe * s + xo * c
            return jnp.stack((re, ro), axis=-1).reshape(x.shape)

        def _heads(t):
            b, n, _ = t.shape
            return t.reshape(b, n, H, DH).transpose(0, 2, 1, 3)

        def _attn(xq, ctx, wq, wkv, wo, bo):
            q = _heads(xq @ wq)
            k, v = jnp.split(ctx @ wkv, 2, axis=-1)
            k = _heads(k)
            v = _heads(v)
            sq, cq = _sincos(q.shape[2], DH)
            sk, ck = _sincos(k.shape[2], DH)
            q = _rope(q, sq, cq)
            k = _rope(k, sk, ck)
            sim = jnp.einsum('bhnd,bhmd->bhnm', q, k) * DH ** (-0.5)
            a = jax.nn.softmax(sim, axis=-1)
            o = jnp.einsum('bhnm,bhmd->bhnd', a, v)
            o = o.transpose(0, 2, 1, 3).reshape(xq.shape[0], xq.shape[1], MID)
            return o @ wo + bo

        def _adaln(x, c, lw, lb, gw, gb, bw, bb):
            g = (c @ gw + gb)[:, None, :]
            bt = (c @ bw + bb)[:, None, :]
            return _ln(x, lw, lb) * (1.0 + g) + bt
        ks = jax.random.split(jax.random.key(seed), 24)
        s = 0.02
        inp = {'x': jax.random.normal(ks[0], (B, N, D), jnp.float32), 'cond': jax.random.normal(ks[1], (B, D), jnp.float32), 'context': jax.random.normal(ks[2], (B, M, DC), jnp.float32), 'ln1_w': jnp.ones((D,), jnp.float32), 'ln1_b': jnp.zeros((D,), jnp.float32), 'g1_w': jax.random.normal(ks[3], (D, D), jnp.float32) * s, 'g1_b': jnp.zeros((D,), jnp.float32), 'b1_w': jax.random.normal(ks[4], (D, D), jnp.float32) * s, 'b1_b': jnp.zeros((D,), jnp.float32), 'ln2_w': jnp.ones((D,), jnp.float32), 'ln2_b': jnp.zeros((D,), jnp.float32), 'g2_w': jax.random.normal(ks[5], (D, D), jnp.float32) * s, 'g2_b': jnp.zeros((D,), jnp.float32), 'b2_w': jax.random.normal(ks[6], (D, D), jnp.float32) * s, 'b2_b': jnp.zeros((D,), jnp.float32), 'sa_wq': jax.random.normal(ks[7], (D, MID), jnp.float32) * s, 'sa_wkv': jax.random.normal(ks[8], (D, 2 * MID), jnp.float32) * s, 'sa_wo': jax.random.normal(ks[9], (MID, D), jnp.float32) * s, 'sa_bo': jnp.zeros((D,), jnp.float32), 'ca_lnc_w': jnp.ones((DC,), jnp.float32), 'ca_lnc_b': jnp.zeros((DC,), jnp.float32), 'ca_wq': jax.random.normal(ks[10], (D, MID), jnp.float32) * s, 'ca_wkv': jax.random.normal(ks[11], (DC, 2 * MID), jnp.float32) * s, 'ca_wo': jax.random.normal(ks[12], (MID, D), jnp.float32) * s, 'ca_bo': jnp.zeros((D,), jnp.float32), 'ff_w1': jax.random.normal(ks[13], (D, MULT * D), jnp.float32) * s, 'ff_b1': jnp.zeros((MULT * D,), jnp.float32), 'ff_w2': jax.random.normal(ks[14], (MULT * D, D), jnp.float32) * s, 'ff_b2': jnp.zeros((D,), jnp.float32)}
        return inp
    _L1_xcond_all = _L1_xcond_setup()
    _L1_xcond_in = {k: v for k, v in _L1_xcond_all.items() if k in ('ln1_w', 'ln1_b', 'g1_w', 'g1_b', 'b1_w', 'b1_b', 'ln2_w', 'ln2_b', 'g2_w', 'g2_b', 'b2_w', 'b2_b', 'sa_wq', 'sa_wkv', 'sa_wo', 'sa_bo', 'ca_lnc_w', 'ca_lnc_b', 'ca_wq', 'ca_wkv', 'ca_wo', 'ca_bo', 'ff_w1', 'ff_b1', 'ff_w2', 'ff_b2')}
    del _L1_xcond_all
    return {'x': x, 'cond_1024': cond_1024, 'ctx_768': ctx_768, 'L0_xcond_n1_w': _L0_xcond_in['n1_w'], 'L0_xcond_n1_b': _L0_xcond_in['n1_b'], 'L0_xcond_n2_w': _L0_xcond_in['n2_w'], 'L0_xcond_n2_b': _L0_xcond_in['n2_b'], 'L0_xcond_n3_w': _L0_xcond_in['n3_w'], 'L0_xcond_n3_b': _L0_xcond_in['n3_b'], 'L0_xcond_q1': _L0_xcond_in['q1'], 'L0_xcond_k1': _L0_xcond_in['k1'], 'L0_xcond_v1': _L0_xcond_in['v1'], 'L0_xcond_o1_w': _L0_xcond_in['o1_w'], 'L0_xcond_o1_b': _L0_xcond_in['o1_b'], 'L0_xcond_q2': _L0_xcond_in['q2'], 'L0_xcond_k2': _L0_xcond_in['k2'], 'L0_xcond_v2': _L0_xcond_in['v2'], 'L0_xcond_o2_w': _L0_xcond_in['o2_w'], 'L0_xcond_o2_b': _L0_xcond_in['o2_b'], 'L0_xcond_ff_w1': _L0_xcond_in['ff_w1'], 'L0_xcond_ff_b1': _L0_xcond_in['ff_b1'], 'L0_xcond_ff_w2': _L0_xcond_in['ff_w2'], 'L0_xcond_ff_b2': _L0_xcond_in['ff_b2'], 'L1_xcond_ln1_w': _L1_xcond_in['ln1_w'], 'L1_xcond_ln1_b': _L1_xcond_in['ln1_b'], 'L1_xcond_g1_w': _L1_xcond_in['g1_w'], 'L1_xcond_g1_b': _L1_xcond_in['g1_b'], 'L1_xcond_b1_w': _L1_xcond_in['b1_w'], 'L1_xcond_b1_b': _L1_xcond_in['b1_b'], 'L1_xcond_ln2_w': _L1_xcond_in['ln2_w'], 'L1_xcond_ln2_b': _L1_xcond_in['ln2_b'], 'L1_xcond_g2_w': _L1_xcond_in['g2_w'], 'L1_xcond_g2_b': _L1_xcond_in['g2_b'], 'L1_xcond_b2_w': _L1_xcond_in['b2_w'], 'L1_xcond_b2_b': _L1_xcond_in['b2_b'], 'L1_xcond_sa_wq': _L1_xcond_in['sa_wq'], 'L1_xcond_sa_wkv': _L1_xcond_in['sa_wkv'], 'L1_xcond_sa_wo': _L1_xcond_in['sa_wo'], 'L1_xcond_sa_bo': _L1_xcond_in['sa_bo'], 'L1_xcond_ca_lnc_w': _L1_xcond_in['ca_lnc_w'], 'L1_xcond_ca_lnc_b': _L1_xcond_in['ca_lnc_b'], 'L1_xcond_ca_wq': _L1_xcond_in['ca_wq'], 'L1_xcond_ca_wkv': _L1_xcond_in['ca_wkv'], 'L1_xcond_ca_wo': _L1_xcond_in['ca_wo'], 'L1_xcond_ca_bo': _L1_xcond_in['ca_bo'], 'L1_xcond_ff_w1': _L1_xcond_in['ff_w1'], 'L1_xcond_ff_b1': _L1_xcond_in['ff_b1'], 'L1_xcond_ff_w2': _L1_xcond_in['ff_w2'], 'L1_xcond_ff_b2': _L1_xcond_in['ff_b2']}

def reference(x, cond_1024, ctx_768, L0_xcond_n1_w, L0_xcond_n1_b, L0_xcond_n2_w, L0_xcond_n2_b, L0_xcond_n3_w, L0_xcond_n3_b, L0_xcond_q1, L0_xcond_k1, L0_xcond_v1, L0_xcond_o1_w, L0_xcond_o1_b, L0_xcond_q2, L0_xcond_k2, L0_xcond_v2, L0_xcond_o2_w, L0_xcond_o2_b, L0_xcond_ff_w1, L0_xcond_ff_b1, L0_xcond_ff_w2, L0_xcond_ff_b2, L1_xcond_ln1_w, L1_xcond_ln1_b, L1_xcond_g1_w, L1_xcond_g1_b, L1_xcond_b1_w, L1_xcond_b1_b, L1_xcond_ln2_w, L1_xcond_ln2_b, L1_xcond_g2_w, L1_xcond_g2_b, L1_xcond_b2_w, L1_xcond_b2_b, L1_xcond_sa_wq, L1_xcond_sa_wkv, L1_xcond_sa_wo, L1_xcond_sa_bo, L1_xcond_ca_lnc_w, L1_xcond_ca_lnc_b, L1_xcond_ca_wq, L1_xcond_ca_wkv, L1_xcond_ca_wo, L1_xcond_ca_bo, L1_xcond_ff_w1, L1_xcond_ff_b1, L1_xcond_ff_w2, L1_xcond_ff_b2):
    import jax
    import jax.numpy as jnp

    def _L0_xcond_ref(x, t, context, n1_w, n1_b, n2_w, n2_b, n3_w, n3_b, q1, k1, v1, o1_w, o1_b, q2, k2, v2, o2_w, o2_b, ff_w1, ff_b1, ff_w2, ff_b2):
        import jax, jax.numpy as jnp
        import numpy as np
        EPS = 1e-05

        def _ada_ln(x, t, W, b):
            emb = t @ W + b
            scale, shift = jnp.split(emb, 2, axis=-1)
            mu = x.mean(-1, keepdims=True)
            var = ((x - mu) ** 2).mean(-1, keepdims=True)
            xn = (x - mu) * jax.lax.rsqrt(var + EPS)
            return xn * (1.0 + scale) + shift

        def _attn(x, ctx, Wq, Wk, Wv, Wo, bo, heads):
            b, n, _ = x.shape
            j = ctx.shape[1]
            q = (x @ Wq).reshape(b, n, heads, -1)
            k = (ctx @ Wk).reshape(b, j, heads, -1)
            v = (ctx @ Wv).reshape(b, j, heads, -1)
            scale = q.shape[-1] ** (-0.5)
            sim = jnp.einsum('bihd,bjhd->bhij', q, k) * scale
            attn = jax.nn.softmax(sim, axis=-1)
            out = jnp.einsum('bhij,bjhd->bihd', attn, v).reshape(b, n, -1)
            return out @ Wo + bo

        def _ff(x, W1, b1, W2, b2):
            p = x @ W1 + b1
            a, gate = jnp.split(p, 2, axis=-1)
            return a * jax.nn.gelu(gate, approximate=False) @ W2 + b2
        H = 16
        h = _ada_ln(x, t, n1_w, n1_b)
        x = _attn(h, h, q1, k1, v1, o1_w, o1_b, H) + x
        h = _ada_ln(x, t, n2_w, n2_b)
        x = _attn(h, context, q2, k2, v2, o2_w, o2_b, H) + x
        h = _ada_ln(x, t, n3_w, n3_b)
        x = _ff(h, ff_w1, ff_b1, ff_w2, ff_b2) + x
        return x

    def _L1_xcond_ref(x, cond, context, ln1_w, ln1_b, g1_w, g1_b, b1_w, b1_b, ln2_w, ln2_b, g2_w, g2_b, b2_w, b2_b, sa_wq, sa_wkv, sa_wo, sa_bo, ca_lnc_w, ca_lnc_b, ca_wq, ca_wkv, ca_wo, ca_bo, ff_w1, ff_b1, ff_w2, ff_b2):
        import jax, jax.numpy as jnp
        import numpy as np
        B, N, M = (2, 256, 128)
        D, H, DH = (256, 16, 64)
        MID = H * DH
        DC = 192
        MULT = 4
        EPS = 1e-05

        def _ln(x, w, b):
            mu = jnp.mean(x, -1, keepdims=True)
            var = jnp.mean((x - mu) ** 2, -1, keepdims=True)
            return (x - mu) * jax.lax.rsqrt(var + EPS) * w + b

        def _sincos(n, d):
            inv = 1.0 / 10000.0 ** (jnp.arange(0, d, 2, dtype=jnp.float32) / d)
            ang = jnp.arange(n, dtype=jnp.float32)[:, None] * inv[None, :]
            return (jnp.sin(ang), jnp.cos(ang))

        def _rope(x, sin, cos):
            s = sin[None, None]
            c = cos[None, None]
            xe = x[..., ::2]
            xo = x[..., 1::2]
            re = xe * c - xo * s
            ro = xe * s + xo * c
            return jnp.stack((re, ro), axis=-1).reshape(x.shape)

        def _heads(t):
            b, n, _ = t.shape
            return t.reshape(b, n, H, DH).transpose(0, 2, 1, 3)

        def _attn(xq, ctx, wq, wkv, wo, bo):
            q = _heads(xq @ wq)
            k, v = jnp.split(ctx @ wkv, 2, axis=-1)
            k = _heads(k)
            v = _heads(v)
            sq, cq = _sincos(q.shape[2], DH)
            sk, ck = _sincos(k.shape[2], DH)
            q = _rope(q, sq, cq)
            k = _rope(k, sk, ck)
            sim = jnp.einsum('bhnd,bhmd->bhnm', q, k) * DH ** (-0.5)
            a = jax.nn.softmax(sim, axis=-1)
            o = jnp.einsum('bhnm,bhmd->bhnd', a, v)
            o = o.transpose(0, 2, 1, 3).reshape(xq.shape[0], xq.shape[1], MID)
            return o @ wo + bo

        def _adaln(x, c, lw, lb, gw, gb, bw, bb):
            g = (c @ gw + gb)[:, None, :]
            bt = (c @ bw + bb)[:, None, :]
            return _ln(x, lw, lb) * (1.0 + g) + bt
        attn_in = _adaln(x, cond, ln1_w, ln1_b, g1_w, g1_b, b1_w, b1_b)
        x = _attn(attn_in, attn_in, sa_wq, sa_wkv, sa_wo, sa_bo) + x
        cross_in = _adaln(x, cond, ln1_w, ln1_b, g1_w, g1_b, b1_w, b1_b)
        ctx_n = _ln(context, ca_lnc_w, ca_lnc_b)
        x = _attn(cross_in, ctx_n, ca_wq, ca_wkv, ca_wo, ca_bo) + x
        ffn_in = _adaln(x, cond, ln2_w, ln2_b, g2_w, g2_b, b2_w, b2_b)
        h = jax.nn.gelu(ffn_in @ ff_w1 + ff_b1, approximate=False)
        x = h @ ff_w2 + ff_b2 + x
        return x
    x = _L0_xcond_ref(x, cond_1024[:, None, :], ctx_768, L0_xcond_n1_w, L0_xcond_n1_b, L0_xcond_n2_w, L0_xcond_n2_b, L0_xcond_n3_w, L0_xcond_n3_b, L0_xcond_q1, L0_xcond_k1, L0_xcond_v1, L0_xcond_o1_w, L0_xcond_o1_b, L0_xcond_q2, L0_xcond_k2, L0_xcond_v2, L0_xcond_o2_w, L0_xcond_o2_b, L0_xcond_ff_w1, L0_xcond_ff_b1, L0_xcond_ff_w2, L0_xcond_ff_b2)
    x = _L1_xcond_ref(x, cond_1024, ctx_768, L1_xcond_ln1_w, L1_xcond_ln1_b, L1_xcond_g1_w, L1_xcond_g1_b, L1_xcond_b1_w, L1_xcond_b1_b, L1_xcond_ln2_w, L1_xcond_ln2_b, L1_xcond_g2_w, L1_xcond_g2_b, L1_xcond_b2_w, L1_xcond_b2_b, L1_xcond_sa_wq, L1_xcond_sa_wkv, L1_xcond_sa_wo, L1_xcond_sa_bo, L1_xcond_ca_lnc_w, L1_xcond_ca_lnc_b, L1_xcond_ca_wq, L1_xcond_ca_wkv, L1_xcond_ca_wo, L1_xcond_ca_bo, L1_xcond_ff_w1, L1_xcond_ff_b1, L1_xcond_ff_w2, L1_xcond_ff_b2)
    return x

_drawn_inputs = setup_inputs


def setup_inputs(seed=0):
    import zlib

    import numpy as np

    out = dict(_drawn_inputs(seed))
    spreads = {'L0_xcond_n1_b': (0.0, 0.367),
     'L0_xcond_n2_b': (0.0, 0.8),
     'L0_xcond_n3_b': (0.0, 0.8),
     'L0_xcond_o1_b': (0.0, 0.1),
     'L0_xcond_o2_b': (0.0, 0.1),
     'L0_xcond_ff_b1': (0.0, 0.464),
     'L0_xcond_ff_b2': (0.0, 0.1),
     'L1_xcond_ln1_w': (1.0, 0.6),
     'L1_xcond_ln1_b': (0.0, 0.389),
     'L1_xcond_g1_b': (0.0, 0.8),
     'L1_xcond_b1_b': (0.0, 0.428),
     'L1_xcond_ln2_w': (1.0, 0.6),
     'L1_xcond_ln2_b': (0.0, 0.723),
     'L1_xcond_g2_b': (0.0, 0.794),
     'L1_xcond_b2_b': (0.0, 0.733),
     'L1_xcond_sa_bo': (0.0, 0.1),
     'L1_xcond_ca_lnc_w': (1.0, 0.6),
     'L1_xcond_ca_lnc_b': (0.0, 0.489),
     'L1_xcond_ca_bo': (0.0, 0.1),
     'L1_xcond_ff_b1': (0.0, 0.1),
     'L1_xcond_ff_b2': (0.0, 0.1)}
    factors = {'L0_xcond_n2_w': 8.0,
     'L0_xcond_q1': 8.0,
     'L0_xcond_k1': 8.0,
     'L0_xcond_q2': 8.0,
     'L0_xcond_k2': 8.0,
     'L1_xcond_g1_w': 3.6,
     'L1_xcond_sa_wq': 8.0,
     'L1_xcond_ca_wq': 8.0}
    for name, (base, spread) in spreads.items():
        noise = np.random.default_rng([zlib.crc32(name.encode()), seed]).standard_normal(out[name].shape)
        drawn = base * np.exp(spread * noise) if base else spread * noise
        out[name] = jnp.asarray(drawn.astype(out[name].dtype))
    for name, factor in factors.items():
        out[name] = (out[name] * factor).astype(out[name].dtype)
    return out
```

```python
import concourse.bass as bass
import numpy as np
from concourse import mybir
from contextlib import ExitStack

F32 = mybir.dt.float32
ALU = mybir.AluOpType
ACT = mybir.ActivationFunctionType
AX = mybir.AxisListType

B, N, D = 4, 512, 256
H, DH = 16, 64
J, DC = 64, 192
P = 128
TT = N // P
KT = D // P
HP = H // 2
CP = DC // 2
JT = N // P
TILES = 2 * TT
FT = 4 * D // P
LNS = 5
EPS = 1e-5
SCALE = DH ** -0.5

SUBLAYERS = ["self0", "cross0", "ff0", "self1", "cross1", "ff1"]
LN_OF = [0, 1, 2, 3, 3, 4]

SCORE_BANKS = [0, 1, 2, 3]
TRANSPOSE_BANKS = [4, 5]
O_BANK = 6
PROJ_BANK = 7


def build(nc, a, out):
    ctx = ExitStack()

    def sb(name, shape):
        return ctx.enter_context(nc.sbuf_tensor(name, shape, F32))

    def sem(name):
        return ctx.enter_context(nc.semaphore(name))

    ident = sb("ident", [P, P])
    rope_cos_q, rope_sin_q = sb("rope_cos_q", [P, N]), sb("rope_sin_q", [P, N])
    rope_cos_k, rope_sin_k = sb("rope_cos_k", [P, N]), sb("rope_sin_k", [P, N])
    cond_t = sb("cond_t", [P, KT, B])
    ada_w_or_probs_t = sb("ada_w_or_probs_t", [P, KT * 10 * D])
    ada_w = ada_w_or_probs_t[:, :].rearrange("p (t c) -> p t c", t=KT)
    probs_t = ada_w_or_probs_t[:, 0:2 * JT * N].rearrange("p (h j i) -> p h j i", h=2, j=JT)
    ada_vec = sb("ada_vec", [P, 28])
    ada_tmp = sb("ada_tmp", [P, 4, KT, B])
    coef = sb("coef", [P, B, LNS, 2, KT])
    coef_b = sb("coef_b", [P, LNS, 2, KT])
    out_bias = sb("out_bias", [P, 6, D])
    ff_bias = sb("ff_bias", [P, 3 * FT])
    ctx_rows = sb("ctx_rows", [J, B, DC])
    ctx_norm = sb("ctx_norm", [J, B, DC])
    ctx_stats, ctx_mv = sb("ctx_stats", [J, B, 6]), sb("ctx_mv", [J, B, 2])
    ctx_rstd = sb("ctx_rstd", [J, B, 1])
    ctx_vec = sb("ctx_vec", [CP, 2, 2])
    ctx_all = sb("ctx_all", [CP, 2, B, 2, J])
    ctx_b = sb("ctx_b", [CP, 2, 2, J])
    x_in, x, xn, y = (sb(n, [P, TT, D]) for n in ("x_in", "x", "xn", "y"))
    stats, mv = sb("stats", [P, TT, 6]), sb("mv", [P, TT, 2])
    totals, apart = sb("totals", [P, TT, 2]), sb("apart", [P, TT, 1])
    rstd = sb("rstd", [P, TT, 1])
    half, eps = sb("half", [P, TT, 1]), sb("eps", [P, TT, 1])
    h_t = sb("h_t", [P, KT, N])
    inner_t = sb("inner_t", [P, HP, N])
    w_out = [sb(f"w_out{k}", [P, HP, D]) for k in range(6)]
    w_qkv = [sb(f"w_qkv{i}", [P, 3, KT, P]) for i in range(2)]
    w_xq = [sb(f"w_xq{i}", [P, KT, P]) for i in range(2)]
    w_xkv = [sb(f"w_xkv{i}", [CP, 2, 2, P]) for i in range(2)]
    w_ff = {2: sb("w_ff0", [P, KT, 8 * D]), 5: sb("w_ff1", [P, KT, 4 * D])}
    q_t = [sb(f"q_t{i}", [P, N]) for i in range(2)]
    k_t = [sb(f"k_t{i}", [P, N]) for i in range(2)]
    v_s = [sb(f"v_s{i}", [P, JT, P]) for i in range(2)]
    k_diag = [sb(f"k_diag{i}", [P, P]) for i in range(2)]
    v_diag = [sb(f"v_diag{i}", [P, P]) for i in range(2)]
    rot = sb("rot", [P, 4, N])
    rot_k = sb("rot_k", [P, 2, J])
    probs = sb("probs", [P, 4, N])
    neg_max, sums, recips = (sb(n, [P, TILES]) for n in ("neg_max", "sums", "recips"))
    gated = sb("gated", [P, 2, N])

    bank = [ctx.enter_context(nc.psum_tensor(f"bank{i}", [P, 512], F32)) for i in range(8)]

    consts_in = sem("consts_in")
    setup_pool, setup_dve, setup_pe = sem("setup_pool"), sem("setup_dve"), sem("setup_pe")
    x_arrived = sem("x_arrived")
    out_stored, y_ready = sem("out_stored"), sem("y_ready")
    batch_ready = sem("batch_ready")

    class Signals:
        pass

    sig = []
    for k, name in enumerate(SUBLAYERS):
        s = Signals()
        s.w_fixed = sem(f"{name}_w_fixed")
        s.stats = sem(f"{name}_stats")
        s.rstd = sem(f"{name}_rstd")
        s.normed = sem(f"{name}_normed")
        s.turned = sem(f"{name}_turned")
        s.h0 = sem(f"{name}_h0")
        s.h1 = sem(f"{name}_h1")
        s.biased = sem(f"{name}_biased")
        s.out_proj = sem(f"{name}_out_proj")
        s.residual = sem(f"{name}_residual")
        if k in (2, 5):
            s.up = sem(f"{name}_up")
            s.gelu = sem(f"{name}_gelu")
            s.hidden = sem(f"{name}_hidden")
        else:
            s.w = [sem(f"{name}_w{i}") for i in range(2)]
            s.q_proj = sem(f"{name}_q_proj")
            s.v_proj = sem(f"{name}_v_proj")
            s.q = sem(f"{name}_q")
            s.k = sem(f"{name}_k")
            s.v = sem(f"{name}_v")
            s.scores = sem(f"{name}_scores")
            s.neg_max = sem(f"{name}_neg_max")
            s.exp = sem(f"{name}_exp")
            s.recip = sem(f"{name}_recip")
            s.probs = sem(f"{name}_probs")
            s.probs_turned = sem(f"{name}_turned_p")
            s.probs_t = sem(f"{name}_probs_t")
            s.o = sem(f"{name}_o")
            s.inner = sem(f"{name}_inner")
            if k in (0, 3):
                s.k_proj = sem(f"{name}_k_proj")
            else:
                s.shifted = sem(f"{name}_shifted")
                s.sums = sem(f"{name}_sums")
            if k >= 3:
                s.q_rot = sem(f"{name}_q_rot")
                s.k_rot = sem(f"{name}_k_rot")
                s.pool = sem(f"{name}_pool")
        sig.append(s)

    SWAP = [i ^ 1 for i in range(32)]
    block = ctx.enter_context(nc.Block())

    CONSTS = [(ident, "ident"), (cond_t, "cond_t"), (ada_w, "ada_w"), (ada_vec, "ada_vec"),
              (ctx_rows, "ctx_rows"), (ctx_vec, "ctx_vec"), (rope_cos_q, "rope_cos_q"),
              (rope_sin_q, "rope_sin_q"), (rope_cos_k, "rope_cos_k"), (rope_sin_k, "rope_sin_k"),
              (out_bias, "out_bias"), (ff_bias, "ff_bias")]

    def full(t):
        return t[tuple(slice(None) for _ in t.shape)]

    @block.sync
    def _(sp):
        def load_pair(k, slot, s):
            if k in (0, 3):
                sp.dma_start(w_qkv[slot][:, :, :, :], a[f"w_qkv{k // 3}"][s, :, :, :, :])\
                    .then_inc(sig[k].w[slot], 16)
            else:
                sp.dma_start(w_xq[slot][:, :, :], a[f"w_xq{k // 3}"][s, :, :, :])\
                    .then_inc(sig[k].w[slot], 16)
                sp.dma_start(w_xkv[slot][:, :, :, :], a[f"w_xkv{k // 3}"][s, :, :, :, :])\
                    .then_inc(sig[k].w[slot], 16)

        sp.dma_start(x_in[:, :, :], a["x"][0, :, :].rearrange("(t p) d -> p t d", p=P))\
            .then_inc(x_arrived, 16)
        for dst, name in CONSTS:
            sp.dma_start(full(dst), a[name]).then_inc(consts_in, 16)
        sp.dma_start(ctx_all[:, 0, :, :, :], a["ctx_t"]).then_inc(consts_in, 16)

        for k in (0, 1):
            for s in range(2):
                load_pair(k, s, s)

        def rounds(b, last):
            for k in (0, 1, 3, 4):
                with sp.Fori(0, 3) as i:
                    for u in range(2):
                        sp.wait_ge(sig[k].v_proj, b * HP + i * 2 + (u + 1))
                        load_pair(k, u, i * 2 + (u + 2))
                if not (last and k >= 3):
                    for u in range(2):
                        sp.wait_ge(sig[k].v_proj, b * HP + (HP - 1 + u))
                        load_pair((k + 3) % 6, u, u)
                if k == 1 and not last:
                    sp.wait_ge(sig[0].biased, b * TT + TT)
                    sp.dma_start(x_in[:, :, :],
                                 a["x"][b + 1, :, :].rearrange("(t p) d -> p t d", p=P))\
                        .then_inc(x_arrived, 16)
            sp.wait_ge(y_ready, b * TT + TT)
            sp.dma_start(out[b, :, :].rearrange("(t p) d -> p t d", p=P), y[:, :, :])\
                .then_inc(out_stored, 16)

        with sp.Fori(0, B - 1) as b:
            rounds(b, False)
        rounds(B - 1, True)
        sp.wait_ge(out_stored, 16 * B + 16)

    @block.gpsimd
    def _(pool):
        pool.memset(half[:, :, :], -0.5).then_inc(setup_pool, 1)
        pool.memset(eps[:, :, :], EPS).then_inc(setup_pool, 1)
        pool.memset(y[:, :, :], 0.0).then_inc(out_stored, 16)
        for i in range(2):
            pool.memset(k_diag[i][:, :], 0.0).then_inc(setup_pool, 1)
            pool.memset(v_diag[i][:, :], 0.0).then_inc(setup_pool, 1)
        pool.wait_ge(setup_dve, 2 * B)
        pool.tensor_scalar(ctx_rstd[:, :, :], ctx_mv[:, :, 1:2], EPS, None, ALU.add)\
            .then_inc(setup_pool, 1)
        pool.wait_ge(setup_pool, 7)
        pool.tensor_tensor(ctx_rstd[:, :, :], ctx_rstd[:, :, :], half[0:J, :, :], ALU.pow)\
            .then_inc(setup_pool, 1)

        def norm(k, b):
            s = sig[k]
            pool.wait_ge(s.stats, b * 8 + 8)
            pool.tensor_tensor(rstd[:, :, :], mv[:, :, 1:2], eps[:, :, :], ALU.add)\
                .then_inc(s.rstd, 1)
            pool.wait_ge(s.rstd, b * 2 + 1)
            pool.tensor_tensor(rstd[:, :, :], rstd[:, :, :], half[:, :, :], ALU.pow)\
                .then_inc(s.rstd, 1)
            pool.wait_ge(s.normed, b * TT + TT)
            src = x_in if k == 0 else x
            for t in range(TT):
                pool.tensor_tensor(x[:, t, :], src[:, t, :], out_bias[:, k, :], ALU.add)\
                    .then_inc(s.biased, 1)

        def rotate(k, dst, n, g):
            s = sig[k]
            done, parts = (s.q, s.q_rot) if n == 0 else (s.k, s.k_rot)
            table = rope_sin_q if n == 0 else rope_sin_k
            pool.wait_ge(parts, g * 2 + 2)
            pool.tensor_tensor(rot[:, 2 * n + 1, :], rot[:, 2 * n + 1, :], table[:, :], ALU.mult)\
                .then_inc(s.pool, 1)
            turns = g * 2 + (1 + n) if k == 3 else g + 1
            pool.wait_ge(s.pool, turns)
            pool.tensor_tensor(dst, rot[:, 2 * n, :], rot[:, 2 * n + 1, :], ALU.add).then_inc(done, 1)

        def project(k, g, par):
            if k == 3:
                rotate(k, q_t[par][:, :], 0, g)
                rotate(k, k_t[par][:, :], 1, g)
            if k == 4:
                rotate(k, q_t[par][:, :], 0, g)

        with pool.Fori(0, B) as b:
            for k in range(6):
                norm(k, b)
                if k in (3, 4):
                    project(k, b * HP, 0)
                    project(k, b * HP + 1, 1)
                    with pool.Fori(0, 3) as i:
                        project(k, b * HP + i * 2 + 2, 0)
                        project(k, b * HP + i * 2 + 3, 1)

    def over_pairs(eng, b, start, body, end):
        start(b * HP)
        body(0, b * HP, 0, True, False)
        with eng.Fori(0, 3) as i:
            body(i * 2 + 1, b * HP + i * 2 + 1, 1, False, False)
            body(i * 2 + 2, b * HP + i * 2 + 2, 0, False, False)
        body(HP - 1, b * HP + (HP - 1), 1, False, True)
        end(b * HP + HP)

    @block.tensor
    def _(pe):
        mm = pe.matmul

        def setup():
            pe.wait_ge(consts_in, 16 * (len(CONSTS) + 1))
            for m in range(10 * KT):
                for kt in range(KT):
                    ins = mm(bank[0][:, m * B:m * B + B], ada_w[:, kt, m * P:m * P + P],
                             cond_t[:, kt, :], start=(kt == 0), stop=(kt == KT - 1))
            ins.then_inc(setup_pe, 1)
            pe.wait_ge(setup_dve, 3 * B)
            for b in range(B):
                for c in range(2):
                    ins = pe.transpose(bank[1][0:CP, (b * 2 + c) * J:(b * 2 + c + 1) * J],
                                       ctx_norm[:, b, c * CP:c * CP + CP], ident[0:J, 0:J])
            ins.then_inc(setup_pe, 1)

        def norm(k, b):
            s = sig[k]
            for c in range(KT):
                for t in range(TT):
                    if c == 0:
                        pe.wait_ge(s.normed, b * TT + (t + 1))
                    ins = pe.transpose(bank[TRANSPOSE_BANKS[c]][:, t * P:t * P + P],
                                       xn[:, t, c * P:c * P + P], ident[:, :])
                ins.then_inc(s.turned, 1)
            pe.wait_ge(s.h0, b + 1)
            pe.wait_ge(s.h1, b + 1)

        def out_proj(k, b, ready, count):
            s = sig[k]
            pe.wait_ge(s.w_fixed, 32 if k in (2, 5) else 16)
            pe.wait_ge(ready, count)
            for t in range(TT):
                for kt in range(HP):
                    ins = mm(bank[t][:, 0:D], inner_t[:, kt, t * P:t * P + P], w_out[k][:, kt, :],
                             start=(kt == 0), stop=(kt == HP - 1))
                ins.then_inc(s.out_proj, 1)

        def project_q(s, par):
            for kt in range(KT):
                ins = mm(bank[PROJ_BANK][:, :], w_qkv[par][:, 0, kt, :], h_t[:, kt, :],
                         start=(kt == 0), stop=(kt == KT - 1))
            ins.then_inc(s.q_proj, 1)

        def project_k(s, par, g):
            pe.wait_ge(s.q if s is sig[0] else s.q_rot, g + 1 if s is sig[0] else g * 2 + 2)
            for kt in range(KT):
                ins = mm(bank[PROJ_BANK][:, :], w_qkv[par][:, 1, kt, :], h_t[:, kt, :],
                         start=(kt == 0), stop=(kt == KT - 1))
            ins.then_inc(s.k_proj, 1)

        def project_v(s, par, g):
            pe.wait_ge(s.k if s is sig[0] else s.k_rot, g + 1 if s is sig[0] else g * 2 + 2)
            for t in range(JT):
                for kt in range(KT):
                    ins = mm(bank[PROJ_BANK][:, t * P:t * P + P], h_t[:, kt, t * P:t * P + P],
                             w_qkv[par][:, 2, kt, :], start=(kt == 0), stop=(kt == KT - 1))
            ins.then_inc(s.v_proj, 1)

        def self_attention(k, b):
            s = sig[k]

            def weights(g_in_slot, par):
                pe.wait_ge(s.w[par], g_in_slot)

            def score(t, g, par, first):
                h, it = divmod(t, TT)
                if not (first and t < 4):
                    pe.wait_ge(s.exp, g * TILES + (t - 3))
                r = slice(DH * h, DH * h + DH)
                mm(bank[SCORE_BANKS[t % 4]][:, :], q_t[par][r, it * P:it * P + P],
                   k_t[par][r, :], start=True, stop=True).then_inc(s.scores, 1)

            def turn(t, g, first):
                pe.wait_ge(s.probs, g * TILES + (t + 1))
                if not (first and t < 2):
                    pe.wait_ge(s.probs_t, g * TILES + (t - 1))
                for jt in range(JT):
                    ins = pe.transpose(bank[TRANSPOSE_BANKS[t % 2]][:, jt * P:jt * P + P],
                                       probs[:, t % 4, jt * P:jt * P + P], ident[:, :])
                ins.then_inc(s.probs_turned, 1)

            def weigh(g, par):
                pe.wait_ge(s.probs_t, g * TILES)
                pe.wait_ge(s.v, g)
                for jt in range(JT):
                    for h in range(2):
                        ins = mm(bank[O_BANK][DH * h:DH * h + DH, :],
                                 v_s[par][:, jt, DH * h:DH * h + DH], probs_t[:, h, jt, :],
                                 start=(jt == 0), stop=(jt == JT - 1))
                ins.then_inc(s.o, 1)

            def start(g):
                weights(b * 64 + 16, 0)
                project_q(s, 0)
                project_k(s, 0, g)
                project_v(s, 0, g)

            def body(sx, g, par, first, last):
                pe.wait_ge(s.q, g + 1)
                pe.wait_ge(s.k, g + 1)
                for t in range(3):
                    score(t, g, par, first)
                if not first:
                    weigh(g, 1 - par)
                for t in range(TILES):
                    turn(t, g, first)
                    if t + 3 < TILES:
                        score(t + 3, g, par, first)
                    if last:
                        continue
                    if t == 1:
                        if first:
                            weights(b * 64 + 16, 1)
                        elif par == 1:
                            weights((g + 1) * 8 + 16, 0)
                        else:
                            weights(g * 8 + 16, 1)
                        pe.wait_ge(s.v, g + 1)
                        project_q(s, 1 - par)
                    if t == 3:
                        project_k(s, 1 - par, g + 1)
                    if t == 5:
                        project_v(s, 1 - par, g + 1)

            def end(g):
                weigh(g, 1)

            over_pairs(pe, b, start, body, end)

        def cross_attention(k, b):
            s, c = sig[k], k // 3

            def front(g, par, slot_count, first):
                pe.wait_ge(s.w[par], slot_count)
                if not first:
                    pe.wait_ge(s.q_rot if k == 4 else s.q, g * 2 if k == 4 else g)
                for kt in range(KT):
                    ins = mm(bank[PROJ_BANK][:, :], w_xq[par][:, kt, :], h_t[:, kt, :],
                             start=(kt == 0), stop=(kt == KT - 1))
                ins.then_inc(s.q_proj, 1)
                if not first:
                    pe.wait_ge(s.v, g)
                for kt in range(2):
                    mm(bank[0][:, 0:J], w_xkv[par][:, 0, kt, :], ctx_b[:, c, kt, :],
                       start=(kt == 0), stop=(kt == 1))
                for h in range(2):
                    for kt in range(2):
                        ins = mm(bank[0][J * h:J * h + J, J + DH * h:J + DH * h + DH],
                                 ctx_b[:, c, kt, :], w_xkv[par][:, 1, kt, DH * h:DH * h + DH],
                                 start=(kt == 0), stop=(kt == 1))
                ins.then_inc(s.v_proj, 1)

            def score(g, par):
                pe.wait_ge(s.q, g + 1)
                pe.wait_ge(s.k, g + 1)
                for it in range(TT):
                    ins = mm(bank[1 + par][:, it * P:it * P + P], q_t[par][:, it * P:it * P + P],
                             k_diag[par][:, :], start=True, stop=True)
                ins.then_inc(s.scores, 1)

            def turn(g, par):
                pe.wait_ge(s.probs, g + 1)
                for it in range(TT):
                    ins = pe.transpose(bank[TRANSPOSE_BANKS[par]][:, it * P:it * P + P],
                                       probs[:, 2 * par, it * P:it * P + P], ident[:, :])
                ins.then_inc(s.probs_turned, 1)

            def weigh(g, par, first):
                pe.wait_ge(s.probs_t, g + 1)
                if not first:
                    pe.wait_ge(s.inner, g)
                mm(bank[O_BANK][:, :], v_diag[par][:, :], probs_t[:, par, 0, :],
                   start=True, stop=True).then_inc(s.o, 1)

            def start(g):
                front(g, 0, b * 128 + 32, True)
                score(g, 0)

            def body(sx, g, par, first, last):
                if not last:
                    slot = (b * 128 + 32 if first else (g + 1) * 16 + 32 if par == 1
                            else g * 16 + 32)
                    front(g + 1, 1 - par, slot, False)
                turn(g, par)
                if not last:
                    score(g + 1, 1 - par)
                weigh(g, par, first)

            over_pairs(pe, b, start, body, lambda g: None)

        def feed_forward(k, b):
            s = sig[k]
            free = s.hidden if k == 2 else s.gelu
            pe.wait_ge(s.w_fixed, 32)
            for m in range(FT):
                if m >= 2:
                    pe.wait_ge(free, b * FT + (m - 1))
                halves = ((0, m), (2, FT + m)) if k == 2 else ((2, m),)
                for base, col in halves:
                    for kt in range(KT):
                        ins = mm(bank[base + m % 2][:, :], w_ff[k][:, kt, col * P:col * P + P],
                                 h_t[:, kt, :], start=(kt == 0), stop=(kt == KT - 1))
                ins.then_inc(s.up, 1)

        setup()
        with pe.Fori(0, B) as b:
            for k in range(6):
                norm(k, b)
                if k in (0, 3):
                    self_attention(k, b)
                    out_proj(k, b, sig[k].inner, b * HP + HP)
                elif k in (1, 4):
                    cross_attention(k, b)
                    out_proj(k, b, sig[k].inner, b * HP + HP)
                else:
                    feed_forward(k, b)
                    out_proj(k, b, sig[k].hidden if k == 2 else sig[k].gelu, b * FT + FT)

    @block.scalar
    def _(act):
        def norm(k, b):
            s = sig[k]
            act.wait_ge(s.turned, b * KT + 1)
            act.activation(h_t[:, 0, :], bank[TRANSPOSE_BANKS[0]][:, :], ACT.Identity,
                           bias=coef_b[:, LN_OF[k], 1, 0:1], scale=coef_b[:, LN_OF[k], 0, 0:1])\
                .then_inc(s.h0, 1)

        def self_attention(k, b):
            s = sig[k]

            def q_out(g, par):
                if k == 0:
                    act.wait_ge(s.q_proj, g + 1)
                    act.activation(q_t[par][:, :], bank[PROJ_BANK][:, :], ACT.Copy, scale=SCALE)\
                        .then_inc(s.q, 1)

            def v_out(g, par):
                act.wait_ge(s.v_proj, g + 1)
                act.activation(v_s[par][:, :, :], bank[PROJ_BANK][:, :], ACT.Copy)\
                    .then_inc(s.v, 1)

            def exp(t, g):
                act.wait_ge(s.neg_max, g * TILES + (t + 1))
                act.activation(probs[:, t % 4, :], bank[SCORE_BANKS[t % 4]][:, :], ACT.Exp,
                               bias=neg_max[:, t:t + 1], scale=1.0, accum_out=sums[:, t:t + 1])\
                    .then_inc(s.exp, 1)

            def turned_out(t, g):
                h, it = divmod(t, TT)
                act.wait_ge(s.probs_turned, g * TILES + (t + 1))
                act.activation(probs_t[:, h, :, it * P:it * P + P],
                               bank[TRANSPOSE_BANKS[t % 2]][:, :].rearrange("p (j i) -> p j i", j=JT),
                               ACT.Copy).then_inc(s.probs_t, 1)

            def start(g):
                q_out(g, 0)
                v_out(g, 0)

            def body(sx, g, par, first, last):
                exp(0, g)
                exp(1, g)
                if not first:
                    act.wait_ge(s.o, g)
                for t in range(TILES):
                    turned_out(t, g)
                    if t + 2 < TILES:
                        exp(t + 2, g)
                    if last:
                        continue
                    if t == 1:
                        q_out(g + 1, 1 - par)
                    if t == 5:
                        v_out(g + 1, 1 - par)

            over_pairs(act, b, start, body, lambda g: None)

        def cross_attention(k, b):
            s = sig[k]

            def q_out(g, par):
                if k == 1:
                    act.wait_ge(s.q_proj, g + 1)
                    act.activation(q_t[par][:, :], bank[PROJ_BANK][:, :], ACT.Copy, scale=SCALE)\
                        .then_inc(s.q, 1)

            def body(sx, g, par, first, last):
                act.wait_ge(s.shifted, g + 1)
                act.activation(probs[:, 2 * par, :], probs[:, 2 * par + 1, :], ACT.Exp)\
                    .then_inc(s.exp, 1)
                if not last:
                    q_out(g + 1, 1 - par)
                act.wait_ge(s.probs_turned, g + 1)
                act.activation(probs_t[:, par, 0, :], bank[TRANSPOSE_BANKS[par]][:, :], ACT.Copy)\
                    .then_inc(s.probs_t, 1)

            over_pairs(act, b, lambda g: q_out(g, 0), body, lambda g: None)

        def feed_forward(k, b):
            s = sig[k]
            for m in range(FT):
                act.wait_ge(s.up, b * FT + (m + 1))
                if k == 2:
                    if m >= 2:
                        act.wait_ge(s.hidden, b * FT + (m - 1))
                    dst, bias = gated[:, m % 2, :], ff_bias[:, FT + m:FT + m + 1]
                else:
                    dst, bias = inner_t[:, m, :], ff_bias[:, 2 * FT + m:2 * FT + m + 1]
                act.activation(dst, bank[2 + m % 2][:, :], ACT.Gelu, bias=bias, scale=1.0)\
                    .then_inc(s.gelu, 1)

        for k in range(6):
            act.dma_start(w_out[k][:, :, :], a[f"w_out{k}"]).then_inc(sig[k].w_fixed, 16)
            if k in (2, 5):
                act.dma_start(w_ff[k][:, :, :], a[f"w_ff{k // 3}"]).then_inc(sig[k].w_fixed, 16)
        with act.Fori(0, B) as b:
            act.wait_ge(batch_ready, b * 2 + 2)
            for k in range(6):
                norm(k, b)
                (self_attention, cross_attention, feed_forward)[k % 3](k, b)

    @block.vector
    def _(dve):
        def setup():
            dve.wait_ge(consts_in, 16 * (len(CONSTS) + 1))
            for b in range(B):
                dve.bn_stats(ctx_stats[:, b, :], ctx_rows[:, b, :]).then_inc(setup_dve, 1)
            dve.wait_ge(setup_dve, B)
            for b in range(B):
                dve.bn_aggr(ctx_mv[:, b, :], ctx_stats[:, b, :]).then_inc(setup_dve, 1)
            dve.wait_ge(setup_dve, 2 * B)
            dve.wait_ge(setup_pool, 8)
            for b in range(B):
                dve.tensor_scalar(ctx_norm[:, b, :], ctx_rows[:, b, :], ctx_mv[:, b, 0:1],
                                  ctx_rstd[:, b, :], ALU.subtract, ALU.mult).then_inc(setup_dve, 1)
            dve.wait_ge(setup_pe, 1)
            emb = bank[0][:, 0:10 * KT * B].rearrange("p (m b) -> p m b", b=B)
            for n in range(3):
                for c in range(KT):
                    v = 4 * n + c
                    dve.tensor_scalar(coef[:, :, n, 0, c], emb[:, v, :], ada_vec[:, v:v + 1], 1.0,
                                      ALU.add, ALU.add)
                    ins = dve.tensor_scalar(coef[:, :, n, 1, c], emb[:, v + 2, :],
                                            ada_vec[:, v + 2:v + 3], None, ALU.add)
            for n in range(2):
                for c in range(KT):
                    m = 12 + 4 * n + c
                    dve.tensor_scalar(ada_tmp[:, 2 * n, c, :], emb[:, m, :], vec(n, c, 0), 1.0,
                                      ALU.add, ALU.add).then_inc(setup_dve, 1)
                    dve.tensor_scalar(ada_tmp[:, 2 * n + 1, c, :], emb[:, m + 2, :], vec(n, c, 1),
                                      None, ALU.add).then_inc(setup_dve, 1)
            dve.wait_ge(setup_dve, 3 * B + 8)
            for n in range(2):
                for c in range(KT):
                    dve.tensor_scalar(coef[:, :, 3 + n, 0, c], ada_tmp[:, 2 * n, c, :], vec(n, c, 2),
                                      None, ALU.mult).then_inc(setup_dve, 1)
                    dve.scalar_tensor_tensor(out=coef[:, :, 3 + n, 1, c],
                                             in0=ada_tmp[:, 2 * n, c, :], scalar=vec(n, c, 3),
                                             in1=ada_tmp[:, 2 * n + 1, c, :], op0=ALU.mult,
                                             op1=ALU.add).then_inc(setup_dve, 1)
            dve.wait_ge(setup_pe, 2)
            turned = bank[1][0:CP, :].rearrange("p (b c j) -> p b c j", b=B, c=2)
            for c in range(2):
                dve.tensor_scalar(ctx_all[:, 1, :, c, :], turned[:, :, c, :], ctx_vec[:, 0, c:c + 1],
                                  ctx_vec[:, 1, c:c + 1], ALU.mult, ALU.add).then_inc(setup_dve, 1)
            dve.wait_ge(setup_dve, 3 * B + 18)

        def vec(n, c, i):
            at = 12 + (n * 4 + i) * KT + c
            return ada_vec[:, at:at + 1]

        def norm(k, b):
            s = sig[k]
            src = x_in if k == 0 else x
            if k == 0:
                dve.wait_ge(x_arrived, b * 16 + 16)
            else:
                dve.wait_ge(sig[k - 1].residual, b * TT + TT)
            for t in range(TT):
                dve.bn_stats(stats[:, t, :], src[:, t, :]).then_inc(s.stats, 1)
            dve.wait_ge(s.stats, b * 8 + 4)
            dve.tensor_tensor(totals[:, :, :], stats[:, :, 1:3], stats[:, :, 4:6], ALU.add)\
                .then_inc(s.stats, 1)
            dve.tensor_tensor(apart[:, :, :], stats[:, :, 1:2], stats[:, :, 4:5], ALU.subtract)\
                .then_inc(s.stats, 1)
            dve.wait_ge(s.stats, b * 8 + 6)
            dve.tensor_scalar(mv[:, :, 0:1], totals[:, :, 0:1], 0.5, None, ALU.mult)
            dve.scalar_tensor_tensor(out=apart[:, :, :], in0=apart[:, :, :], scalar=0.25,
                                     in1=apart[:, :, :], op0=ALU.mult, op1=ALU.mult)\
                .then_inc(s.stats, 1)
            dve.wait_ge(s.stats, b * 8 + 7)
            dve.scalar_tensor_tensor(out=mv[:, :, 1:2], in0=totals[:, :, 1:2], scalar=1.0 / D,
                                     in1=apart[:, :, :], op0=ALU.mult, op1=ALU.add)\
                .then_inc(s.stats, 1)
            dve.wait_ge(s.stats, b * 8 + 8)
            dve.wait_ge(s.rstd, b * 2 + 2)
            for t in range(TT):
                dve.tensor_scalar(xn[:, t, :], src[:, t, :], mv[:, t, 0:1], rstd[:, t, :],
                                  ALU.subtract, ALU.mult).then_inc(s.normed, 1)
            dve.wait_ge(s.turned, b * KT + 2)
            dve.tensor_scalar(h_t[:, 1, :], bank[TRANSPOSE_BANKS[1]][:, :],
                              coef_b[:, LN_OF[k], 0, 1:2], coef_b[:, LN_OF[k], 1, 1:2],
                              ALU.mult, ALU.add).then_inc(s.h1, 1)

        def residual(k, b):
            s = sig[k]
            dve.wait_ge(s.biased, b * TT + TT)
            if k == 5:
                dve.wait_ge(out_stored, b * 16 + 16)
            dst = y if k == 5 else x
            for t in range(TT):
                dve.wait_ge(s.out_proj, b * TT + (t + 1))
                dve.tensor_tensor(dst[:, t, :], bank[t][:, 0:D], x[:, t, :], ALU.add)\
                    .then_inc(y_ready if k == 5 else s.residual, 1)

        def self_attention(k, b):
            s = sig[k]

            def rope(n, g, first=False):
                src = bank[PROJ_BANK][:, :]
                parts = s.q_rot if n == 0 else s.k_rot
                dve.wait_ge(s.q_proj if n == 0 else s.k_proj, g + 1)
                if not first:
                    dve.wait_ge(s.q if n == 0 else s.k, g)
                dve.tensor_tensor(rot[:, 2 * n, :], src, (rope_cos_q if n == 0 else rope_cos_k)[:, :],
                                  ALU.mult).then_inc(parts, 1)
                dve.stream_shuffle(rot[:, 2 * n + 1, :], src, SWAP).then_inc(parts, 1)

            def q_out(g, first=False):
                if k == 3:
                    rope(0, g, first)

            def k_out(g, par, first=False):
                if k == 3:
                    rope(1, g, first)
                else:
                    dve.wait_ge(s.k_proj, g + 1)
                    dve.tensor_copy(k_t[par][:, :], bank[PROJ_BANK][:, :]).then_inc(s.k, 1)

            def row_max(t, g):
                dve.wait_ge(s.scores, g * TILES + (t + 1))
                dve.tensor_reduce(neg_max[:, t:t + 1], bank[SCORE_BANKS[t % 4]][:, :], AX.X,
                                  ALU.max, negate=True).then_inc(s.neg_max, 1)

            def normalise(t, g):
                dve.wait_ge(s.exp, g * TILES + (t + 1))
                dve.reciprocal(recips[:, t:t + 1], sums[:, t:t + 1]).then_inc(s.recip, 1)
                dve.wait_ge(s.recip, g * TILES + (t + 1))
                dve.tensor_scalar(probs[:, t % 4, :], probs[:, t % 4, :], recips[:, t:t + 1], None,
                                  ALU.mult).then_inc(s.probs, 1)

            def o_out(sx, g):
                dve.wait_ge(s.o, g)
                dve.tensor_copy(inner_t[:, sx, :], bank[O_BANK][:, :]).then_inc(s.inner, 1)

            def start(g):
                q_out(g, True)
                k_out(g, 0, True)

            def body(sx, g, par, first, last):
                row_max(0, g)
                row_max(1, g)
                for t in range(TILES):
                    normalise(t, g)
                    if t + 2 < TILES:
                        row_max(t + 2, g)
                    if t == 0 and not first:
                        o_out(sx - 1, g)
                    if last:
                        continue
                    if t == 1:
                        q_out(g + 1)
                    if t == 3:
                        k_out(g + 1, 1 - par)

            over_pairs(dve, b, start, body, lambda g: o_out(HP - 1, g))

        def cross_attention(k, b):
            s = sig[k]

            def q_out(g, first=False):
                if k == 4:
                    dve.wait_ge(s.q_proj, g + 1)
                    if not first:
                        dve.wait_ge(s.q, g)
                    dve.tensor_tensor(rot[:, 0, :], bank[PROJ_BANK][:, :], rope_cos_q[:, :],
                                      ALU.mult).then_inc(s.q_rot, 1)
                    dve.stream_shuffle(rot[:, 1, :], bank[PROJ_BANK][:, :], SWAP)\
                        .then_inc(s.q_rot, 1)

            def kv_out(g, par):
                dve.wait_ge(s.v_proj, g + 1)
                src = bank[0][:, 0:J]
                if k == 4:
                    dve.tensor_tensor(rot_k[:, 0, :], src, rope_cos_k[:, 0:J], ALU.mult)\
                        .then_inc(s.k_rot, 1)
                    dve.stream_shuffle(rot_k[:, 1, :], src, SWAP).then_inc(s.k_rot, 1)
                    dve.wait_ge(s.k_rot, g * 3 + 2)
                    dve.tensor_tensor(rot_k[:, 1, :], rot_k[:, 1, :], rope_sin_k[:, 0:J],
                                      ALU.mult).then_inc(s.k_rot, 1)
                    dve.wait_ge(s.k_rot, g * 3 + 3)
                for h in range(2):
                    r = slice(DH * h, DH * h + DH)
                    c = slice(J * h, J * h + J)
                    if k == 4:
                        ins = dve.tensor_tensor(k_diag[par][r, c], rot_k[r, 0, :], rot_k[r, 1, :],
                                                ALU.add)
                    else:
                        ins = dve.tensor_copy(k_diag[par][r, c], bank[0][r, 0:J])
                    if h == 1:
                        ins.then_inc(s.k, 1)
                for h in range(2):
                    r = slice(J * h, J * h + J)
                    ins = dve.tensor_copy(v_diag[par][r, DH * h:DH * h + DH],
                                          bank[0][r, J + DH * h:J + DH * h + DH])
                ins.then_inc(s.v, 1)

            rows = 2 * TT

            def by_row(ap):
                return ap.rearrange("p (r j) -> p r j", j=J)

            def across(ap):
                return ap.unsqueeze(2).to_broadcast([P, rows, J])

            def softmax_a(g, par):
                dve.wait_ge(s.scores, g + 1)
                dve.tensor_reduce(neg_max[:, :], by_row(bank[1 + par][:, :]), AX.X, ALU.max,
                                  negate=True).then_inc(s.neg_max, 1)
                dve.wait_ge(s.neg_max, g + 1)
                dve.tensor_tensor(by_row(probs[:, 2 * par + 1, :]), by_row(bank[1 + par][:, :]),
                                  across(neg_max[:, :]), ALU.add).then_inc(s.shifted, 1)

            def softmax_b(g, par):
                dve.wait_ge(s.exp, g + 1)
                dve.tensor_reduce(sums[:, :], by_row(probs[:, 2 * par, :]), AX.X, ALU.add)\
                    .then_inc(s.sums, 1)
                dve.wait_ge(s.sums, g + 1)
                dve.reciprocal(recips[:, :], sums[:, :]).then_inc(s.recip, 1)
                dve.wait_ge(s.recip, g + 1)
                dve.tensor_tensor(by_row(probs[:, 2 * par, :]), by_row(probs[:, 2 * par, :]),
                                  across(recips[:, :]), ALU.mult).then_inc(s.probs, 1)

            def o_out(sx, g):
                dve.wait_ge(s.o, g)
                dve.tensor_copy(inner_t[:, sx, :], bank[O_BANK][:, :]).then_inc(s.inner, 1)

            def start(g):
                q_out(g, True)
                kv_out(g, 0)

            def body(sx, g, par, first, last):
                softmax_a(g, par)
                if not first:
                    o_out(sx - 1, g)
                if not last:
                    q_out(g + 1)
                    kv_out(g + 1, 1 - par)
                softmax_b(g, par)

            over_pairs(dve, b, start, body, lambda g: o_out(HP - 1, g))

        def feed_forward(k, b):
            s = sig[k]
            if k == 5:
                return
            for m in range(FT):
                dve.wait_ge(s.gelu, b * FT + (m + 1))
                dve.scalar_tensor_tensor(out=inner_t[:, m, :], in0=bank[m % 2][:, :],
                                         scalar=ff_bias[:, m:m + 1], in1=gated[:, m % 2, :],
                                         op0=ALU.add, op1=ALU.mult).then_inc(s.hidden, 1)

        setup()
        with dve.Fori(0, B) as b:
            dve.tensor_copy(coef_b[:, :, :, :], coef[:, b, :, :, :]).then_inc(batch_ready, 1)
            dve.tensor_copy(ctx_b[:, :, :, :], ctx_all[:, :, b, :, :]).then_inc(batch_ready, 1)
            dve.wait_ge(batch_ready, b * 2 + 2)
            for k in range(6):
                norm(k, b)
                (self_attention, cross_attention, feed_forward)[k % 3](k, b)
                residual(k, b)

    ctx.close()


def kernel(**inputs):
    import concourse.bacc as bacc
    from concourse.bass_utils import run_bass_kernel_spmd

    g = {n: np.asarray(v) for n, v in inputs.items()}
    l0 = {n[9:]: v for n, v in g.items() if n.startswith("L0_xcond_")}
    l1 = {n[9:]: v for n, v in g.items() if n.startswith("L1_xcond_")}

    def by_partition(w, p=P):
        return w.reshape(-1, p, w.shape[1]).transpose(1, 0, 2)

    def columns(v, p=P):
        return v.reshape(-1, p).T

    def per_pair(w, p=P):
        t = w.shape[0] // p
        return w.reshape(t, p, HP, P).transpose(2, 1, 0, 3)

    inner = H * DH
    arrays = {
        "x": g["x"],
        "cond_t": by_partition(g["cond_1024"].T),
        "ctx_rows": g["ctx_768"].transpose(1, 0, 2),
        "ctx_t": g["ctx_768"].reshape(B, J, 2, CP).transpose(3, 0, 2, 1),
        "ident": np.eye(P, dtype=np.float32),
        "ada_w": by_partition(np.concatenate(
            [l0["n1_w"], l0["n2_w"], l0["n3_w"], l1["g1_w"], l1["b1_w"], l1["g2_w"], l1["b2_w"]], 1)),
        "ada_vec": np.concatenate([columns(v) for v in (
            l0["n1_b"], l0["n2_b"], l0["n3_b"], l1["g1_b"], l1["b1_b"], l1["ln1_w"], l1["ln1_b"],
            l1["g2_b"], l1["b2_b"], l1["ln2_w"], l1["ln2_b"])], 1),
        "ctx_vec": np.stack([columns(l1["ca_lnc_w"], CP), columns(l1["ca_lnc_b"], CP)], 1),
        "out_bias": np.broadcast_to(np.stack(
            [l0["o1_b"], l0["o2_b"], l0["ff_b2"], l1["sa_bo"], l1["ca_bo"], l1["ff_b2"]]), (P, 6, D)),
        "ff_bias": np.concatenate([columns(l0["ff_b1"]), columns(l1["ff_b1"])], 1),
        "w_ff0": by_partition(l0["ff_w1"]),
        "w_ff1": by_partition(l1["ff_w1"]),
    }
    for k, w in enumerate((l0["o1_w"], l0["o2_w"], l0["ff_w2"], l1["sa_wo"], l1["ca_wo"],
                           l1["ff_w2"])):
        arrays[f"w_out{k}"] = by_partition(w)
    qkv = [(l0["q1"], l0["k1"], l0["v1"]),
           (l1["sa_wq"], l1["sa_wkv"][:, :inner], l1["sa_wkv"][:, inner:])]
    cross = [(l0["q2"], l0["k2"], l0["v2"]),
             (l1["ca_wq"], l1["ca_wkv"][:, :inner], l1["ca_wkv"][:, inner:])]
    for n in range(2):
        arrays[f"w_qkv{n}"] = np.stack([per_pair(w) for w in qkv[n]], 2)
        arrays[f"w_xq{n}"] = per_pair(cross[n][0])
        arrays[f"w_xkv{n}"] = np.stack([per_pair(w, CP) for w in cross[n][1:]], 2)

    inv = np.float32(1.0) / np.power(np.float32(10000.0),
                                     np.arange(0, DH, 2, dtype=np.float32) / np.float32(DH))
    angle = np.arange(N, dtype=np.float32)[:, None] * inv[None, :].astype(np.float32)
    cos, sin = (np.tile(np.repeat(f(angle), 2, 1).T, (2, 1)) for f in (np.cos, np.sin))
    sign = np.tile(np.array([-1.0, 1.0], np.float32), P // 2)[:, None]
    for name, table in (("cos", cos), ("sin", sin * sign)):
        arrays[f"rope_{name}_q"] = (table * np.float32(SCALE)).astype(np.float32)
        arrays[f"rope_{name}_k"] = table.astype(np.float32)
    arrays = {n: np.ascontiguousarray(v) for n, v in arrays.items()}

    nc = bacc.Bacc("TRN2", target_bir_lowering=False, num_devices=1)
    aps = {n: nc.dram_tensor(n + "_dram", v.shape, F32, kind="ExternalInput").ap()
           for n, v in arrays.items()}
    out = nc.dram_tensor("out_dram", (B, N, D), F32, kind="ExternalOutput").ap()
    build(nc, aps, out)
    r = run_bass_kernel_spmd(nc, [{n + "_dram": v for n, v in arrays.items()}], core_ids=[0])
    return r.results[0]["out_dram"]
```

```python
import concourse.bass as bass
import numpy as np
from concourse import mybir
from contextlib import ExitStack

F32 = mybir.dt.float32
ALU = mybir.AluOpType
ACT = mybir.ActivationFunctionType
AX = mybir.AxisListType

B, N, D = 4, 512, 256
H, DH = 16, 64
J, DC = 64, 192
P = 128
TT = N // P
KT = D // P
HP = H // 2
CP = DC // 2
JT = N // P
TILES = 2 * TT
FT = 4 * D // P
LNS = 5
EPS = 1e-5
SCALE = DH ** -0.5

SUBLAYERS = ["self0", "cross0", "ff0", "self1", "cross1", "ff1"]
LN_OF = [0, 1, 2, 3, 3, 4]

PAIR = 2
JOBS = [(k, which) for k in range(6) for which in range(PAIR)]

SCORE_BANKS = [0, 1, 2, 3]
OUT_BANKS = [1, 2, 3, 2]
OUT_READ = {0: 0, 1: 1, 2: 4, 3: 3}
TRANSPOSE_BANKS = [4, 5]
O_BANK = 6
PROJ_BANK = 7


def build(nc, a, out):
    ctx = ExitStack()
    nc.disable_value_cache = True

    def sb(name, shape):
        return ctx.enter_context(nc.sbuf_tensor(name, shape, F32))

    def sem(name):
        return ctx.enter_context(nc.semaphore(name))

    ident = sb("ident", [P, P])
    rope_cos_q, rope_sin_q = sb("rope_cos_q", [P, N]), sb("rope_sin_q", [P, N])
    rope_cos_k, rope_sin_k = sb("rope_cos_k", [P, N]), sb("rope_sin_k", [P, N])
    cond_t = sb("cond_t", [P, KT, B])
    ada_w_or_probs_t = sb("ada_w_or_probs_t", [P, KT * 10 * D])
    ada_w = ada_w_or_probs_t[:, :].rearrange("p (t c) -> p t c", t=KT)
    probs_t = ada_w_or_probs_t[:, 0:2 * JT * N].rearrange("p (h j i) -> p h j i", h=2, j=JT)
    ada_vec = sb("ada_vec", [P, 28])
    ada_tmp = sb("ada_tmp", [P, 4, KT, B])
    coef = sb("coef", [P, B, LNS, 2, KT])
    coef_b = [sb(f"coef_b{i}", [P, LNS, 2, KT]) for i in range(PAIR)]
    out_bias = sb("out_bias", [P, 6, D])
    ff_bias = sb("ff_bias", [P, 3 * FT])
    ctx_rows = sb("ctx_rows", [J, B, DC])
    ctx_norm = sb("ctx_norm", [J, B, DC])
    ctx_stats, ctx_mv = sb("ctx_stats", [J, B, 6]), sb("ctx_mv", [J, B, 2])
    ctx_rstd = sb("ctx_rstd", [J, B, 1])
    ctx_vec = sb("ctx_vec", [CP, 2, 2])
    ctx_all = sb("ctx_all", [CP, 2, B, 2, J])
    ctx_b = [sb(f"ctx_b{i}", [CP, 2, 2, J]) for i in range(PAIR)]
    xs = [sb(f"x{i}", [P, TT, D]) for i in range(PAIR)]
    xn, y = sb("xn", [P, TT, D]), sb("y", [P, TT, D])
    stats, mv = sb("stats", [P, TT, 6]), sb("mv", [P, TT, 2])
    totals, apart = sb("totals", [P, TT, 2]), sb("apart", [P, TT, 1])
    rstd = sb("rstd", [P, TT, 1])
    half, eps = sb("half", [P, TT, 1]), sb("eps", [P, TT, 1])
    h_ts = [sb(f"h_t{i}", [P, KT, N]) for i in range(PAIR)]
    inner_t = sb("inner_t", [P, HP, N])
    w_out = [sb(f"w_out{k}", [P, HP, D]) for k in range(6)]
    w_qkv = [sb(f"w_qkv{i}", [P, 3, KT, P]) for i in range(2)]
    w_xq = [sb(f"w_xq{i}", [P, KT, P]) for i in range(2)]
    w_xkv = [sb(f"w_xkv{i}", [CP, 2, 2, P]) for i in range(2)]
    w_ff = {2: sb("w_ff0", [P, KT, 8 * D]), 5: sb("w_ff1", [P, KT, 4 * D])}
    q_t = [sb(f"q_t{i}", [P, N]) for i in range(2)]
    k_t = [sb(f"k_t{i}", [P, N]) for i in range(2)]
    v_s = [sb(f"v_s{i}", [P, JT, P]) for i in range(2)]
    k_diag = [sb(f"k_diag{i}", [P, P]) for i in range(2)]
    v_diag = [sb(f"v_diag{i}", [P, P]) for i in range(2)]
    rot = sb("rot", [P, 4, N])
    rot_k = sb("rot_k", [P, 2, J])
    probs = sb("probs", [P, 4, N])
    neg_max, sums, recips = (sb(n, [P, TILES]) for n in ("neg_max", "sums", "recips"))
    gated = sb("gated", [P, 2, N])

    bank = [ctx.enter_context(nc.psum_tensor(f"bank{i}", [P, 512], F32)) for i in range(8)]

    consts_in = sem("consts_in")
    setup_pool, setup_dve, setup_pe = sem("setup_pool"), sem("setup_dve"), sem("setup_pe")
    x_arrived = [sem(f"x_arrived{i}") for i in range(PAIR)]
    out_stored, y_ready = sem("out_stored"), sem("y_ready")
    batch_ready = sem("batch_ready")

    class Signals:
        pass

    sig = []
    for k, name in enumerate(SUBLAYERS):
        s = Signals()
        s.w_fixed = sem(f"{name}_w_fixed")
        s.stats = sem(f"{name}_stats")
        s.rstd = sem(f"{name}_rstd")
        s.normed = sem(f"{name}_normed")
        s.turned = sem(f"{name}_turned")
        s.h0 = sem(f"{name}_h0")
        s.h1 = sem(f"{name}_h1")
        s.biased = sem(f"{name}_biased")
        s.out_proj = sem(f"{name}_out_proj")
        s.residual = sem(f"{name}_residual")
        if k in (2, 5):
            s.up = sem(f"{name}_up")
            s.gelu = sem(f"{name}_gelu")
            s.hidden = sem(f"{name}_hidden")
        else:
            s.w = [sem(f"{name}_w{i}") for i in range(2)]
            s.q_proj = sem(f"{name}_q_proj")
            s.v_proj = sem(f"{name}_v_proj")
            s.q = sem(f"{name}_q")
            s.k = sem(f"{name}_k")
            s.v = sem(f"{name}_v")
            s.scores = sem(f"{name}_scores")
            s.neg_max = sem(f"{name}_neg_max")
            s.exp = sem(f"{name}_exp")
            s.recip = sem(f"{name}_recip")
            s.probs = sem(f"{name}_probs")
            s.probs_turned = sem(f"{name}_turned_p")
            s.probs_t = sem(f"{name}_probs_t")
            s.o = sem(f"{name}_o")
            s.inner = sem(f"{name}_inner")
            if k in (0, 3):
                s.k_proj = sem(f"{name}_k_proj")
            else:
                s.shifted = sem(f"{name}_shifted")
                s.sums = sem(f"{name}_sums")
            if k >= 3:
                s.q_rot = sem(f"{name}_q_rot")
                s.k_rot = sem(f"{name}_k_rot")
                s.pool = sem(f"{name}_pool")
        sig.append(s)

    SWAP = [i ^ 1 for i in range(32)]
    block = ctx.enter_context(nc.Block())

    CONSTS = [(ident, "ident"), (cond_t, "cond_t"), (ada_w, "ada_w"), (ada_vec, "ada_vec"),
              (ctx_rows, "ctx_rows"), (ctx_vec, "ctx_vec"), (rope_cos_q, "rope_cos_q"),
              (rope_sin_q, "rope_sin_q"), (rope_cos_k, "rope_cos_k"), (rope_sin_k, "rope_sin_k"),
              (out_bias, "out_bias"), (ff_bias, "ff_bias")]

    def full(t):
        return t[tuple(slice(None) for _ in t.shape)]

    @block.sync
    def _(sp):
        def load_pair(k, slot, s):
            if k in (0, 3):
                sp.dma_start(w_qkv[slot][:, :, :, :], a[f"w_qkv{k // 3}"][s, :, :, :, :])\
                    .then_inc(sig[k].w[slot], 16)
            else:
                sp.dma_start(w_xq[slot][:, :, :], a[f"w_xq{k // 3}"][s, :, :, :])\
                    .then_inc(sig[k].w[slot], 16)
                sp.dma_start(w_xkv[slot][:, :, :, :], a[f"w_xkv{k // 3}"][s, :, :, :, :])\
                    .then_inc(sig[k].w[slot], 16)

        def load_x(which, b):
            sp.dma_start(xs[which][:, :, :], a["x"][b, :, :].rearrange("(t p) d -> p t d", p=P))\
                .then_inc(x_arrived[which], 16)

        for which in range(PAIR):
            load_x(which, which)
        for dst, name in CONSTS:
            sp.dma_start(full(dst), a[name]).then_inc(consts_in, 16)
        sp.dma_start(ctx_all[:, 0, :, :, :], a["ctx_t"]).then_inc(consts_in, 16)

        for k in (0, 1):
            for s in range(2):
                load_pair(k, s, s)

        for first_b in range(0, B, PAIR):
            for k, which in JOBS:
                b = first_b + which
                if k in (0, 1, 3, 4):
                    with sp.Fori(0, 3) as i:
                        for u in range(2):
                            sp.wait_ge(sig[k].v_proj, i * 2 + (b * HP + u + 1))
                            load_pair(k, u, i * 2 + (u + 2))
                    nxt = k if which == 0 else (k + 3) % 6
                    if not (k >= 3 and b == B - 1):
                        for u in range(2):
                            sp.wait_ge(sig[k].v_proj, b * HP + HP - 1 + u)
                            load_pair(nxt, u, u)
                if k == 5:
                    sp.wait_ge(y_ready, b * TT + TT)
                    sp.dma_start(out[b, :, :].rearrange("(t p) d -> p t d", p=P), y[:, :, :])\
                        .then_inc(out_stored, 16)
                    if b + PAIR < B:
                        load_x(which, b + PAIR)
        sp.wait_ge(out_stored, 16 * B + 16)

    @block.gpsimd
    def _(pool):
        pool.memset(half[:, :, :], -0.5).then_inc(setup_pool, 1)
        pool.memset(eps[:, :, :], EPS).then_inc(setup_pool, 1)
        pool.memset(y[:, :, :], 0.0).then_inc(out_stored, 16)
        for i in range(2):
            pool.memset(k_diag[i][:, :], 0.0).then_inc(setup_pool, 1)
            pool.memset(v_diag[i][:, :], 0.0).then_inc(setup_pool, 1)
        pool.wait_ge(setup_dve, 2 * B)
        pool.tensor_scalar(ctx_rstd[:, :, :], ctx_mv[:, :, 1:2], EPS, None, ALU.add)\
            .then_inc(setup_pool, 1)
        pool.wait_ge(setup_pool, 7)
        pool.tensor_tensor(ctx_rstd[:, :, :], ctx_rstd[:, :, :], half[0:J, :, :], ALU.pow)\
            .then_inc(setup_pool, 1)

        def norm_std(k, which, b):
            s = sig[k]
            pool.wait_ge(s.stats, b * 8 + 8)
            pool.tensor_tensor(rstd[:, :, :], mv[:, :, 1:2], eps[:, :, :], ALU.add)\
                .then_inc(s.rstd, 1)
            pool.wait_ge(s.rstd, b * 2 + 1)
            pool.tensor_tensor(rstd[:, :, :], rstd[:, :, :], half[:, :, :], ALU.pow)\
                .then_inc(s.rstd, 1)

        def add_bias(k, which, b):
            x = xs[which]
            pool.wait_ge(sig[k].normed, b * TT + TT)
            for t in range(TT):
                pool.tensor_tensor(x[:, t, :], x[:, t, :], out_bias[:, k, :], ALU.add)\
                    .then_inc(sig[k].biased, 1)

        def rotate(k, dst, n, g):
            s = sig[k]
            done, parts = (s.q, s.q_rot) if n == 0 else (s.k, s.k_rot)
            table = rope_sin_q if n == 0 else rope_sin_k
            pool.wait_ge(parts, g * 2 + 2)
            pool.tensor_tensor(rot[:, 2 * n + 1, :], rot[:, 2 * n + 1, :], table[:, :], ALU.mult)\
                .then_inc(s.pool, 1)
            turns = g * 2 + (1 + n) if k == 3 else g + 1
            pool.wait_ge(s.pool, turns)
            pool.tensor_tensor(dst, rot[:, 2 * n, :], rot[:, 2 * n + 1, :], ALU.add).then_inc(done, 1)

        def project(k, g, par):
            if k == 3:
                rotate(k, q_t[par][:, :], 0, g)
                rotate(k, k_t[par][:, :], 1, g)
            if k == 4:
                rotate(k, q_t[par][:, :], 0, g)

        def job_at(n, pp):
            k, which = JOBS[n]
            return k, which, pp * PAIR + which

        with pool.Fori(0, B // PAIR) as pp:
            norm_std(*job_at(0, pp))
            add_bias(*job_at(0, pp))
            for n in range(len(JOBS)):
                k, which, b = job_at(n, pp)
                if k in (3, 4):
                    project(k, b * HP, 0)
                    project(k, b * HP + 1, 1)
                if n + 1 < len(JOBS):
                    norm_std(*job_at(n + 1, pp))
                if k in (3, 4):
                    with pool.Fori(0, 3) as i:
                        project(k, b * HP + i * 2 + 2, 0)
                        project(k, b * HP + i * 2 + 3, 1)
                if n + 1 < len(JOBS):
                    add_bias(*job_at(n + 1, pp))

    def over_pairs(eng, b, body, end):
        body(0, b * HP, 0, True, False)
        with eng.Fori(0, 3) as i:
            body(i * 2 + 1, b * HP + i * 2 + 1, 1, False, False)
            body(i * 2 + 2, b * HP + i * 2 + 2, 0, False, False)
        body(HP - 1, b * HP + (HP - 1), 1, False, True)
        end(b * HP + HP)

    def over_jobs(eng, begin, start, run, finish):
        with eng.Fori(0, B // PAIR) as pp:
            jobs = [(k, which, pp * PAIR + which) for k, which in JOBS]
            begin(*jobs[0])
            start(*jobs[0])
            for n, job in enumerate(jobs):
                nxt = jobs[n + 1] if n + 1 < len(jobs) else None
                run(job, nxt, jobs[n - 1] if n else None)
                if nxt:
                    start(*nxt)
                finish(*job)

    @block.tensor
    def _(pe):
        mm = pe.matmul

        def setup():
            pe.wait_ge(consts_in, 16 * (len(CONSTS) + 1))
            for m in range(10 * KT):
                for kt in range(KT):
                    ins = mm(bank[0][:, m * B:m * B + B], ada_w[:, kt, m * P:m * P + P],
                             cond_t[:, kt, :], start=(kt == 0), stop=(kt == KT - 1))
            ins.then_inc(setup_pe, 1)
            pe.wait_ge(setup_dve, 3 * B)
            for b in range(B):
                for c in range(2):
                    ins = pe.transpose(bank[1][0:CP, (b * 2 + c) * J:(b * 2 + c + 1) * J],
                                       ctx_norm[:, b, c * CP:c * CP + CP], ident[0:J, 0:J])
            ins.then_inc(setup_pe, 1)

        def norm_turn(k, b, c):
            s = sig[k]
            for t in range(TT):
                if c == 0:
                    pe.wait_ge(s.normed, b * TT + (t + 1))
                ins = pe.transpose(bank[TRANSPOSE_BANKS[c]][:, t * P:t * P + P],
                                   xn[:, t, c * P:c * P + P], ident[:, :])
            ins.then_inc(s.turned, 1)

        def h_ready(k, b):
            pe.wait_ge(sig[k].h0, b + 1)
            pe.wait_ge(sig[k].h1, b + 1)

        def out_free(prev, banks):
            if prev:
                k, _, b = prev
                tiles = max(OUT_READ[i] for i in banks)
                if tiles:
                    pe.wait_ge(y_ready if k == 5 else sig[k].residual, b * TT + tiles)

        def out_proj(k, which, b):
            s = sig[k]
            pe.wait_ge(s.w_fixed, 32 if k in (2, 5) else 16)
            if k % 3 == 2:
                pe.wait_ge(s.hidden if k == 2 else s.gelu, b * FT + FT)
            else:
                pe.wait_ge(s.inner, b * HP + HP)
            for t in range(TT):
                if t == 3:
                    pe.wait_ge(y_ready if k == 5 else s.residual, b * TT + 2)
                for kt in range(HP):
                    ins = mm(bank[OUT_BANKS[t]][:, 0:D], inner_t[:, kt, t * P:t * P + P],
                             w_out[k][:, kt, :], start=(kt == 0), stop=(kt == HP - 1))
                ins.then_inc(s.out_proj, 1)

        def project_q(s, par, h_t, to=PROJ_BANK):
            for kt in range(KT):
                ins = mm(bank[to][:, :], w_qkv[par][:, 0, kt, :], h_t[:, kt, :],
                         start=(kt == 0), stop=(kt == KT - 1))
            ins.then_inc(s.q_proj, 1)

        def project_k(s, par, h_t, to=PROJ_BANK):
            for kt in range(KT):
                ins = mm(bank[to][:, :], w_qkv[par][:, 1, kt, :], h_t[:, kt, :],
                         start=(kt == 0), stop=(kt == KT - 1))
            ins.then_inc(s.k_proj, 1)

        def project_v(s, par, h_t, to=PROJ_BANK):
            for t in range(JT):
                for kt in range(KT):
                    ins = mm(bank[to][:, t * P:t * P + P], h_t[:, kt, t * P:t * P + P],
                             w_qkv[par][:, 2, kt, :], start=(kt == 0), stop=(kt == KT - 1))
            ins.then_inc(s.v_proj, 1)

        def self_start(k, which, b):
            s, h_t = sig[k], h_ts[which]
            h_ready(k, b)
            pe.wait_ge(s.w[0], b * 64 + 16)
            project_q(s, 0, h_t)
            project_k(s, 0, h_t, TRANSPOSE_BANKS[0])
            project_v(s, 0, h_t, TRANSPOSE_BANKS[1])

        def self_attention(job, nxt, prev):
            k, which, b = job
            s, h_t = sig[k], h_ts[which]

            def read(done, rotated, g):
                if k == 3:
                    pe.wait_ge(rotated, g * 2 + 2)
                else:
                    pe.wait_ge(done, g + 1)

            def score(t, g, par, first):
                h, it = divmod(t, TT)
                if not (first and t < 4):
                    pe.wait_ge(s.exp, g * TILES + (t - 3))
                else:
                    out_free(prev, [SCORE_BANKS[t]])
                r = slice(DH * h, DH * h + DH)
                mm(bank[SCORE_BANKS[t % 4]][:, :], q_t[par][r, it * P:it * P + P],
                   k_t[par][r, :], start=True, stop=True).then_inc(s.scores, 1)

            def turn(t, g, first):
                pe.wait_ge(s.probs, g * TILES + (t + 1))
                if not (first and t < 2):
                    pe.wait_ge(s.probs_t, g * TILES + (t - 1))
                elif t == 1:
                    pe.wait_ge(s.v, g + 1)
                for jt in range(JT):
                    ins = pe.transpose(bank[TRANSPOSE_BANKS[t % 2]][:, jt * P:jt * P + P],
                                       probs[:, t % 4, jt * P:jt * P + P], ident[:, :])
                ins.then_inc(s.probs_turned, 1)

            def weigh(g, par):
                pe.wait_ge(s.probs_t, g * TILES)
                pe.wait_ge(s.v, g)
                for jt in range(JT):
                    for h in range(2):
                        ins = mm(bank[O_BANK][DH * h:DH * h + DH, :],
                                 v_s[par][:, jt, DH * h:DH * h + DH], probs_t[:, h, jt, :],
                                 start=(jt == 0), stop=(jt == JT - 1))
                ins.then_inc(s.o, 1)

            def body(sx, g, par, first, last):
                pe.wait_ge(s.q, g + 1)
                pe.wait_ge(s.k, g + 1)
                for t in range(3):
                    score(t, g, par, first)
                if not first:
                    weigh(g, 1 - par)
                for t in range(TILES):
                    turn(t, g, first)
                    if t + 3 < TILES:
                        score(t + 3, g, par, first)
                    if last:
                        continue
                    if t == 1:
                        pe.wait_ge(s.w[1 - par], b * 64 + 16 if first else
                                   (g + 1) * 8 + 16 if par == 1 else g * 8 + 16)
                        pe.wait_ge(s.v, g + 1)
                        project_q(s, 1 - par, h_t)
                    if t == 3:
                        read(s.q, s.q_rot if k == 3 else None, g + 1)
                        project_k(s, 1 - par, h_t)
                    if t == 5:
                        read(s.k, s.k_rot if k == 3 else None, g + 1)
                        project_v(s, 1 - par, h_t)

            def end(g):
                if nxt:
                    for c in range(KT):
                        pe.wait_ge(s.probs_t, g * TILES - 1 + c)
                        norm_turn(nxt[0], nxt[2], c)
                weigh(g, 1)

            over_pairs(pe, b, body, end)

        def front(k, which, g, par, slot_count, first):
            s, c, h_t = sig[k], k // 3, h_ts[which]
            pe.wait_ge(s.w[par], slot_count)
            if not first:
                pe.wait_ge(s.q_rot if k == 4 else s.q, g * 2 if k == 4 else g)
            for kt in range(KT):
                ins = mm(bank[PROJ_BANK][:, :], w_xq[par][:, kt, :], h_t[:, kt, :],
                         start=(kt == 0), stop=(kt == KT - 1))
            ins.then_inc(s.q_proj, 1)
            if not first:
                pe.wait_ge(s.v, g)
                pe.wait_ge(s.k, g)
            for kt in range(2):
                mm(bank[0][:, 0:J], w_xkv[par][:, 0, kt, :], ctx_b[which][:, c, kt, :],
                   start=(kt == 0), stop=(kt == 1))
            for h in range(2):
                for kt in range(2):
                    ins = mm(bank[0][J * h:J * h + J, J + DH * h:J + DH * h + DH],
                             ctx_b[which][:, c, kt, :], w_xkv[par][:, 1, kt, DH * h:DH * h + DH],
                             start=(kt == 0), stop=(kt == 1))
            ins.then_inc(s.v_proj, 1)

        def cross_start(k, which, b):
            h_ready(k, b)
            front(k, which, b * HP, 0, b * 128 + 32, True)

        def cross_attention(job, nxt, prev):
            k, which, b = job
            s = sig[k]

            def score(g, par):
                pe.wait_ge(s.q, g + 1)
                pe.wait_ge(s.k, g + 1)
                for it in range(TT):
                    ins = mm(bank[1 + par][:, it * P:it * P + P], q_t[par][:, it * P:it * P + P],
                             k_diag[par][:, :], start=True, stop=True)
                ins.then_inc(s.scores, 1)

            def turn(g, par):
                pe.wait_ge(s.probs, g + 1)
                for it in range(TT):
                    ins = pe.transpose(bank[TRANSPOSE_BANKS[par]][:, it * P:it * P + P],
                                       probs[:, 2 * par, it * P:it * P + P], ident[:, :])
                ins.then_inc(s.probs_turned, 1)

            def weigh(g, par):
                pe.wait_ge(s.probs_t, g + 1)
                pe.wait_ge(s.v, g + 1)
                mm(bank[O_BANK][:, :], v_diag[par][:, :], probs_t[:, par, 0, :],
                   start=True, stop=True).then_inc(s.o, 1)

            def body(sx, g, par, first, last):
                if first:
                    out_free(prev, [1])
                score(g, par)
                if not first:
                    turn(g - 1, 1 - par)
                if first:
                    out_free(prev, [2])
                if not last:
                    slot = (b * 128 + 32 if first else (g + 1) * 16 + 32 if par == 1
                            else g * 16 + 32)
                    front(k, which, g + 1, 1 - par, slot, False)
                if not first:
                    weigh(g - 1, 1 - par)

            def end(g):
                turn(g - 1, 1)
                if nxt:
                    norm_turn(nxt[0], nxt[2], 0)
                    pe.wait_ge(s.probs_t, g)
                    norm_turn(nxt[0], nxt[2], 1)
                weigh(g - 1, 1)

            over_pairs(pe, b, body, end)

        def feed_forward(job, nxt, prev):
            k, which, b = job
            s, h_t = sig[k], h_ts[which]
            free = s.hidden if k == 2 else s.gelu
            pe.wait_ge(s.w_fixed, 32)
            for m in range(FT):
                banks = [m % 2, 3 - m % 2]
                if m < 2:
                    out_free(prev, banks if k == 2 or m == 1 else banks[:1])
                else:
                    pe.wait_ge(free, b * FT + (m - 1))
                halves = (m, FT + m) if k == 2 else (m,)
                for to, col in zip(banks, halves):
                    for kt in range(KT):
                        ins = mm(bank[to][:, :], w_ff[k][:, kt, col * P:col * P + P],
                                 h_t[:, kt, :], start=(kt == 0), stop=(kt == KT - 1))
                ins.then_inc(s.up, 1)
            if nxt:
                for c in range(KT):
                    norm_turn(nxt[0], nxt[2], c)

        def begin(k, which, b):
            for c in range(KT):
                norm_turn(k, b, c)

        setup()
        over_jobs(pe, begin,
                  lambda k, which, b: (self_start, cross_start, lambda *_: h_ready(k, b))[k % 3]
                  (k, which, b),
                  lambda job, nxt, prev: (self_attention, cross_attention, feed_forward)[job[0] % 3]
                  (job, nxt, prev), out_proj)

    @block.scalar
    def _(act):
        def h_out(k, which, b):
            s = sig[k]
            act.wait_ge(s.turned, b * KT + 1)
            act.activation(h_ts[which][:, 0, :], bank[TRANSPOSE_BANKS[0]][:, :], ACT.Identity,
                           bias=coef_b[which][:, LN_OF[k], 1, 0:1],
                           scale=coef_b[which][:, LN_OF[k], 0, 0:1]).then_inc(s.h0, 1)

        def q_out(k, g, par):
            if k < 3:
                act.wait_ge(sig[k].q_proj, g + 1)
                act.activation(q_t[par][:, :], bank[PROJ_BANK][:, :], ACT.Copy, scale=SCALE)\
                    .then_inc(sig[k].q, 1)

        def v_out(k, g, par, src=PROJ_BANK):
            act.wait_ge(sig[k].v_proj, g + 1)
            act.activation(v_s[par][:, :, :], bank[src][:, :], ACT.Copy).then_inc(sig[k].v, 1)

        def self_start(k, which, b):
            q_out(k, b * HP, 0)
            v_out(k, b * HP, 0, TRANSPOSE_BANKS[1])

        def self_attention(job, nxt):
            k, which, b = job
            s = sig[k]

            def exp(t, g):
                act.wait_ge(s.neg_max, g * TILES + (t + 1))
                act.activation(probs[:, t % 4, :], bank[SCORE_BANKS[t % 4]][:, :], ACT.Exp,
                               bias=neg_max[:, t:t + 1], scale=1.0, accum_out=sums[:, t:t + 1])\
                    .then_inc(s.exp, 1)

            def turned_out(t, g):
                h, it = divmod(t, TT)
                act.wait_ge(s.probs_turned, g * TILES + (t + 1))
                act.activation(probs_t[:, h, :, it * P:it * P + P],
                               bank[TRANSPOSE_BANKS[t % 2]][:, :].rearrange("p (j i) -> p j i", j=JT),
                               ACT.Copy).then_inc(s.probs_t, 1)

            def body(sx, g, par, first, last):
                exp(0, g)
                exp(1, g)
                if not first:
                    act.wait_ge(s.o, g)
                for t in range(TILES):
                    turned_out(t, g)
                    if t + 2 < TILES:
                        exp(t + 2, g)
                    if last:
                        continue
                    if t == 2:
                        q_out(k, g + 1, 1 - par)
                    if t == 6:
                        v_out(k, g + 1, 1 - par)

            over_pairs(act, b, body, lambda g: h_out(*nxt) if nxt else None)

        def ctx_v_out(k, g, par):
            act.wait_ge(sig[k].v_proj, g + 1)
            act.wait_ge(sig[k].k, g + 1)
            for h in range(2):
                r = slice(J * h, J * h + J)
                ins = act.activation(v_diag[par][r, DH * h:DH * h + DH],
                                     bank[0][r, J + DH * h:J + DH * h + DH], ACT.Copy)
            ins.then_inc(sig[k].v, 1)

        def cross_start(k, which, b):
            q_out(k, b * HP, 0)
            ctx_v_out(k, b * HP, 0)

        def cross_attention(job, nxt):
            k, which, b = job
            s = sig[k]

            def turned_out(g, par):
                act.wait_ge(s.probs_turned, g + 1)
                act.activation(probs_t[:, par, 0, :], bank[TRANSPOSE_BANKS[par]][:, :], ACT.Copy)\
                    .then_inc(s.probs_t, 1)

            def o_out(sx, g):
                act.wait_ge(s.o, g)
                act.activation(inner_t[:, sx, :], bank[O_BANK][:, :], ACT.Copy).then_inc(s.inner, 1)

            def body(sx, g, par, first, last):
                if not first:
                    turned_out(g - 1, 1 - par)
                act.wait_ge(s.shifted, g + 1)
                act.activation(probs[:, 2 * par, :], probs[:, 2 * par + 1, :], ACT.Exp)\
                    .then_inc(s.exp, 1)
                if not last:
                    q_out(k, g + 1, 1 - par)
                if not first:
                    o_out(sx - 1, g)
                if not last:
                    ctx_v_out(k, g + 1, 1 - par)

            def end(g):
                turned_out(g - 1, 1)
                if nxt:
                    h_out(*nxt)
                o_out(HP - 1, g)

            over_pairs(act, b, body, end)

        def feed_forward(job, nxt):
            k, which, b = job
            s = sig[k]
            for m in range(FT):
                act.wait_ge(s.up, b * FT + (m + 1))
                if k == 2:
                    if m >= 2:
                        act.wait_ge(s.hidden, b * FT + (m - 1))
                    dst, src = gated[:, m % 2, :], bank[3 - m % 2]
                    bias = ff_bias[:, FT + m:FT + m + 1]
                else:
                    dst, src = inner_t[:, m, :], bank[m % 2]
                    bias = ff_bias[:, 2 * FT + m:2 * FT + m + 1]
                act.activation(dst, src[:, :], ACT.Gelu, bias=bias, scale=1.0).then_inc(s.gelu, 1)
            if nxt:
                h_out(*nxt)

        for k in range(6):
            act.dma_start(w_out[k][:, :, :], a[f"w_out{k}"]).then_inc(sig[k].w_fixed, 16)
            if k in (2, 5):
                act.dma_start(w_ff[k][:, :, :], a[f"w_ff{k // 3}"]).then_inc(sig[k].w_fixed, 16)

        def begin(k, which, b):
            act.wait_ge(batch_ready, b * 2 + 4)
            h_out(k, which, b)

        over_jobs(act, begin,
                  lambda k, which, b: (self_start, cross_start, lambda *_: None)[k % 3](k, which, b),
                  lambda job, nxt, prev: (self_attention, cross_attention, feed_forward)[job[0] % 3]
                  (job, nxt), lambda *_: None)

    @block.vector
    def _(dve):
        def setup():
            dve.wait_ge(consts_in, 16 * (len(CONSTS) + 1))
            for b in range(B):
                dve.bn_stats(ctx_stats[:, b, :], ctx_rows[:, b, :]).then_inc(setup_dve, 1)
            dve.wait_ge(setup_dve, B)
            for b in range(B):
                dve.bn_aggr(ctx_mv[:, b, :], ctx_stats[:, b, :]).then_inc(setup_dve, 1)
            dve.wait_ge(setup_dve, 2 * B)
            dve.wait_ge(setup_pool, 8)
            for b in range(B):
                dve.tensor_scalar(ctx_norm[:, b, :], ctx_rows[:, b, :], ctx_mv[:, b, 0:1],
                                  ctx_rstd[:, b, :], ALU.subtract, ALU.mult).then_inc(setup_dve, 1)
            dve.wait_ge(setup_pe, 1)
            emb = bank[0][:, 0:10 * KT * B].rearrange("p (m b) -> p m b", b=B)
            for n in range(3):
                for c in range(KT):
                    v = 4 * n + c
                    dve.tensor_scalar(coef[:, :, n, 0, c], emb[:, v, :], ada_vec[:, v:v + 1], 1.0,
                                      ALU.add, ALU.add)
                    ins = dve.tensor_scalar(coef[:, :, n, 1, c], emb[:, v + 2, :],
                                            ada_vec[:, v + 2:v + 3], None, ALU.add)
            for n in range(2):
                for c in range(KT):
                    m = 12 + 4 * n + c
                    dve.tensor_scalar(ada_tmp[:, 2 * n, c, :], emb[:, m, :], vec(n, c, 0), 1.0,
                                      ALU.add, ALU.add).then_inc(setup_dve, 1)
                    dve.tensor_scalar(ada_tmp[:, 2 * n + 1, c, :], emb[:, m + 2, :], vec(n, c, 1),
                                      None, ALU.add).then_inc(setup_dve, 1)
            dve.wait_ge(setup_dve, 3 * B + 8)
            for n in range(2):
                for c in range(KT):
                    dve.tensor_scalar(coef[:, :, 3 + n, 0, c], ada_tmp[:, 2 * n, c, :], vec(n, c, 2),
                                      None, ALU.mult).then_inc(setup_dve, 1)
                    dve.scalar_tensor_tensor(out=coef[:, :, 3 + n, 1, c],
                                             in0=ada_tmp[:, 2 * n, c, :], scalar=vec(n, c, 3),
                                             in1=ada_tmp[:, 2 * n + 1, c, :], op0=ALU.mult,
                                             op1=ALU.add).then_inc(setup_dve, 1)
            dve.wait_ge(setup_pe, 2)
            turned = bank[1][0:CP, :].rearrange("p (b c j) -> p b c j", b=B, c=2)
            for c in range(2):
                dve.tensor_scalar(ctx_all[:, 1, :, c, :], turned[:, :, c, :], ctx_vec[:, 0, c:c + 1],
                                  ctx_vec[:, 1, c:c + 1], ALU.mult, ALU.add).then_inc(setup_dve, 1)
            dve.wait_ge(setup_dve, 3 * B + 18)

        def vec(n, c, i):
            at = 12 + (n * 4 + i) * KT + c
            return ada_vec[:, at:at + 1]

        def norm_stats(k, which, b):
            s, x = sig[k], xs[which]
            if k == 0:
                dve.wait_ge(x_arrived[which], (b + (2 - which)) * 8)
            else:
                dve.wait_ge(sig[k - 1].residual, b * TT + TT)
            for t in range(TT):
                dve.bn_stats(stats[:, t, :], x[:, t, :]).then_inc(s.stats, 1)
            dve.wait_ge(s.stats, b * 8 + 4)
            dve.tensor_tensor(totals[:, :, :], stats[:, :, 1:3], stats[:, :, 4:6], ALU.add)\
                .then_inc(s.stats, 1)
            dve.tensor_tensor(apart[:, :, :], stats[:, :, 1:2], stats[:, :, 4:5], ALU.subtract)\
                .then_inc(s.stats, 1)
            dve.wait_ge(s.stats, b * 8 + 6)
            dve.tensor_scalar(mv[:, :, 0:1], totals[:, :, 0:1], 0.5, None, ALU.mult)
            dve.scalar_tensor_tensor(out=apart[:, :, :], in0=apart[:, :, :], scalar=0.25,
                                     in1=apart[:, :, :], op0=ALU.mult, op1=ALU.mult)\
                .then_inc(s.stats, 1)
            dve.wait_ge(s.stats, b * 8 + 7)
            dve.scalar_tensor_tensor(out=mv[:, :, 1:2], in0=totals[:, :, 1:2], scalar=1.0 / D,
                                     in1=apart[:, :, :], op0=ALU.mult, op1=ALU.add)\
                .then_inc(s.stats, 1)

        def norm_apply(k, which, b):
            s, x = sig[k], xs[which]
            dve.wait_ge(s.rstd, b * 2 + 2)
            for t in range(TT):
                dve.tensor_scalar(xn[:, t, :], x[:, t, :], mv[:, t, 0:1], rstd[:, t, :],
                                  ALU.subtract, ALU.mult).then_inc(s.normed, 1)

        def h_out(k, which, b):
            s = sig[k]
            dve.wait_ge(s.turned, b * KT + 2)
            dve.tensor_scalar(h_ts[which][:, 1, :], bank[TRANSPOSE_BANKS[1]][:, :],
                              coef_b[which][:, LN_OF[k], 0, 1:2],
                              coef_b[which][:, LN_OF[k], 1, 1:2], ALU.mult, ALU.add)\
                .then_inc(s.h1, 1)

        def residual(k, which, b):
            s, x = sig[k], xs[which]
            dve.wait_ge(s.biased, b * TT + TT)
            if k == 5:
                dve.wait_ge(out_stored, b * 16 + 16)
            dst = y if k == 5 else x
            for t in range(TT):
                dve.wait_ge(s.out_proj, b * TT + (t + 1))
                dve.tensor_tensor(dst[:, t, :], bank[OUT_BANKS[t]][:, 0:D], x[:, t, :], ALU.add)\
                    .then_inc(y_ready if k == 5 else s.residual, 1)

        def rope(k, n, g, first, src):
            s = sig[k]
            parts = s.q_rot if n == 0 else s.k_rot
            dve.wait_ge(s.q_proj if n == 0 else s.k_proj, g + 1)
            if not first:
                dve.wait_ge(s.q if n == 0 else s.k, g)
            dve.tensor_tensor(rot[:, 2 * n, :], bank[src][:, :],
                              (rope_cos_q if n == 0 else rope_cos_k)[:, :], ALU.mult)\
                .then_inc(parts, 1)
            dve.stream_shuffle(rot[:, 2 * n + 1, :], bank[src][:, :], SWAP).then_inc(parts, 1)

        def self_q_out(k, g, first=False):
            if k == 3:
                rope(k, 0, g, first, PROJ_BANK)

        def self_k_out(k, g, par, first=False, src=PROJ_BANK):
            if k == 3:
                rope(k, 1, g, first, src)
            else:
                dve.wait_ge(sig[k].k_proj, g + 1)
                dve.tensor_copy(k_t[par][:, :], bank[src][:, :]).then_inc(sig[k].k, 1)

        def self_start(k, which, b):
            self_q_out(k, b * HP, True)
            self_k_out(k, b * HP, 0, True, TRANSPOSE_BANKS[0])

        def self_attention(job, nxt):
            k, which, b = job
            s = sig[k]

            def row_max(t, g):
                dve.wait_ge(s.scores, g * TILES + (t + 1))
                dve.tensor_reduce(neg_max[:, t:t + 1], bank[SCORE_BANKS[t % 4]][:, :], AX.X,
                                  ALU.max, negate=True).then_inc(s.neg_max, 1)

            def normalise(t, g):
                dve.wait_ge(s.exp, g * TILES + (t + 1))
                dve.reciprocal(recips[:, t:t + 1], sums[:, t:t + 1]).then_inc(s.recip, 1)
                dve.wait_ge(s.recip, g * TILES + (t + 1))
                dve.tensor_scalar(probs[:, t % 4, :], probs[:, t % 4, :], recips[:, t:t + 1], None,
                                  ALU.mult).then_inc(s.probs, 1)

            def o_out(sx, g):
                dve.wait_ge(s.o, g)
                dve.tensor_copy(inner_t[:, sx, :], bank[O_BANK][:, :]).then_inc(s.inner, 1)

            def body(sx, g, par, first, last):
                row_max(0, g)
                row_max(1, g)
                for t in range(TILES):
                    normalise(t, g)
                    if t + 2 < TILES:
                        row_max(t + 2, g)
                    if t == 0 and not first:
                        o_out(sx - 1, g)
                    if first and nxt and t == 3:
                        norm_stats(*nxt)
                    if last and nxt and t == 3:
                        norm_apply(*nxt)
                    if last:
                        continue
                    if t == 2:
                        self_q_out(k, g + 1)
                    if t == 4:
                        self_k_out(k, g + 1, 1 - par)

            def end(g):
                if nxt:
                    h_out(*nxt)
                o_out(HP - 1, g)

            over_pairs(dve, b, body, end)

        def cross_q_out(k, g, first=False):
            if k == 4:
                s = sig[k]
                dve.wait_ge(s.q_proj, g + 1)
                if not first:
                    dve.wait_ge(s.q, g)
                dve.tensor_tensor(rot[:, 0, :], bank[PROJ_BANK][:, :], rope_cos_q[:, :],
                                  ALU.mult).then_inc(s.q_rot, 1)
                dve.stream_shuffle(rot[:, 1, :], bank[PROJ_BANK][:, :], SWAP).then_inc(s.q_rot, 1)

        def ctx_k_out(k, g, par):
            s = sig[k]
            dve.wait_ge(s.v_proj, g + 1)
            src = bank[0][:, 0:J]
            if k == 4:
                dve.tensor_tensor(rot_k[:, 0, :], src, rope_cos_k[:, 0:J], ALU.mult)\
                    .then_inc(s.k_rot, 1)
                dve.stream_shuffle(rot_k[:, 1, :], src, SWAP).then_inc(s.k_rot, 1)
                dve.wait_ge(s.k_rot, g * 3 + 2)
                dve.tensor_tensor(rot_k[:, 1, :], rot_k[:, 1, :], rope_sin_k[:, 0:J], ALU.mult)\
                    .then_inc(s.k_rot, 1)
                dve.wait_ge(s.k_rot, g * 3 + 3)
            for h in range(2):
                r = slice(DH * h, DH * h + DH)
                c = slice(J * h, J * h + J)
                if k == 4:
                    ins = dve.tensor_tensor(k_diag[par][r, c], rot_k[r, 0, :], rot_k[r, 1, :],
                                            ALU.add)
                else:
                    ins = dve.tensor_copy(k_diag[par][r, c], bank[0][r, 0:J])
            ins.then_inc(s.k, 1)

        def cross_start(k, which, b):
            cross_q_out(k, b * HP, True)
            ctx_k_out(k, b * HP, 0)

        def cross_attention(job, nxt):
            k, which, b = job
            s = sig[k]
            rows = 2 * TT

            def by_row(ap):
                return ap.rearrange("p (r j) -> p r j", j=J)

            def across(ap):
                return ap.unsqueeze(2).to_broadcast([P, rows, J])

            def softmax_a(g, par):
                dve.wait_ge(s.scores, g + 1)
                dve.tensor_reduce(neg_max[:, :], by_row(bank[1 + par][:, :]), AX.X, ALU.max,
                                  negate=True).then_inc(s.neg_max, 1)
                dve.wait_ge(s.neg_max, g + 1)
                dve.tensor_tensor(by_row(probs[:, 2 * par + 1, :]), by_row(bank[1 + par][:, :]),
                                  across(neg_max[:, :]), ALU.add).then_inc(s.shifted, 1)

            def softmax_b(g, par):
                dve.wait_ge(s.exp, g + 1)
                dve.tensor_reduce(sums[:, :], by_row(probs[:, 2 * par, :]), AX.X, ALU.add)\
                    .then_inc(s.sums, 1)
                dve.wait_ge(s.sums, g + 1)
                dve.reciprocal(recips[:, :], sums[:, :]).then_inc(s.recip, 1)
                dve.wait_ge(s.recip, g + 1)
                dve.tensor_tensor(by_row(probs[:, 2 * par, :]), by_row(probs[:, 2 * par, :]),
                                  across(recips[:, :]), ALU.mult).then_inc(s.probs, 1)

            def body(sx, g, par, first, last):
                softmax_a(g, par)
                if last and nxt:
                    norm_apply(*nxt)
                softmax_b(g, par)
                if not last:
                    cross_q_out(k, g + 1)
                    ctx_k_out(k, g + 1, 1 - par)
                if first and nxt:
                    norm_stats(*nxt)

            over_pairs(dve, b, body, lambda g: h_out(*nxt) if nxt else None)

        def feed_forward(job, nxt):
            k, which, b = job
            s = sig[k]
            if nxt:
                norm_stats(*nxt)
            for m in range(FT):
                if k == 2:
                    dve.wait_ge(s.gelu, b * FT + (m + 1))
                    dve.scalar_tensor_tensor(out=inner_t[:, m, :], in0=bank[m % 2][:, :],
                                             scalar=ff_bias[:, m:m + 1], in1=gated[:, m % 2, :],
                                             op0=ALU.add, op1=ALU.mult).then_inc(s.hidden, 1)
                if m == 3 and nxt:
                    norm_apply(*nxt)
            if nxt:
                h_out(*nxt)

        setup()

        def begin(k, which, b):
            for i in range(PAIR):
                dve.tensor_copy(coef_b[i][:, :, :, :], coef[:, b + i, :, :, :])\
                    .then_inc(batch_ready, 1)
                dve.tensor_copy(ctx_b[i][:, :, :, :], ctx_all[:, :, b + i, :, :])\
                    .then_inc(batch_ready, 1)
            dve.wait_ge(batch_ready, b * 2 + 4)
            norm_stats(k, which, b)
            norm_apply(k, which, b)
            h_out(k, which, b)

        over_jobs(dve, begin,
                  lambda k, which, b: (self_start, cross_start, lambda *_: None)[k % 3](k, which, b),
                  lambda job, nxt, prev: (self_attention, cross_attention, feed_forward)[job[0] % 3]
                  (job, nxt), residual)

    ctx.close()


def kernel(**inputs):
    import concourse.bacc as bacc
    from concourse.bass_utils import run_bass_kernel_spmd

    g = {n: np.asarray(v) for n, v in inputs.items()}
    l0 = {n[9:]: v for n, v in g.items() if n.startswith("L0_xcond_")}
    l1 = {n[9:]: v for n, v in g.items() if n.startswith("L1_xcond_")}

    def by_partition(w, p=P):
        return w.reshape(-1, p, w.shape[1]).transpose(1, 0, 2)

    def columns(v, p=P):
        return v.reshape(-1, p).T

    def per_pair(w, p=P):
        t = w.shape[0] // p
        return w.reshape(t, p, HP, P).transpose(2, 1, 0, 3)

    inner = H * DH
    arrays = {
        "x": g["x"],
        "cond_t": by_partition(g["cond_1024"].T),
        "ctx_rows": g["ctx_768"].transpose(1, 0, 2),
        "ctx_t": g["ctx_768"].reshape(B, J, 2, CP).transpose(3, 0, 2, 1),
        "ident": np.eye(P, dtype=np.float32),
        "ada_w": by_partition(np.concatenate(
            [l0["n1_w"], l0["n2_w"], l0["n3_w"], l1["g1_w"], l1["b1_w"], l1["g2_w"], l1["b2_w"]], 1)),
        "ada_vec": np.concatenate([columns(v) for v in (
            l0["n1_b"], l0["n2_b"], l0["n3_b"], l1["g1_b"], l1["b1_b"], l1["ln1_w"], l1["ln1_b"],
            l1["g2_b"], l1["b2_b"], l1["ln2_w"], l1["ln2_b"])], 1),
        "ctx_vec": np.stack([columns(l1["ca_lnc_w"], CP), columns(l1["ca_lnc_b"], CP)], 1),
        "out_bias": np.broadcast_to(np.stack(
            [l0["o1_b"], l0["o2_b"], l0["ff_b2"], l1["sa_bo"], l1["ca_bo"], l1["ff_b2"]]), (P, 6, D)),
        "ff_bias": np.concatenate([columns(l0["ff_b1"]), columns(l1["ff_b1"])], 1),
        "w_ff0": by_partition(l0["ff_w1"]),
        "w_ff1": by_partition(l1["ff_w1"]),
    }
    for k, w in enumerate((l0["o1_w"], l0["o2_w"], l0["ff_w2"], l1["sa_wo"], l1["ca_wo"],
                           l1["ff_w2"])):
        arrays[f"w_out{k}"] = by_partition(w)
    qkv = [(l0["q1"], l0["k1"], l0["v1"]),
           (l1["sa_wq"], l1["sa_wkv"][:, :inner], l1["sa_wkv"][:, inner:])]
    cross = [(l0["q2"], l0["k2"], l0["v2"]),
             (l1["ca_wq"], l1["ca_wkv"][:, :inner], l1["ca_wkv"][:, inner:])]
    for n in range(2):
        arrays[f"w_qkv{n}"] = np.stack([per_pair(w) for w in qkv[n]], 2)
        arrays[f"w_xq{n}"] = per_pair(cross[n][0])
        arrays[f"w_xkv{n}"] = np.stack([per_pair(w, CP) for w in cross[n][1:]], 2)

    inv = np.float32(1.0) / np.power(np.float32(10000.0),
                                     np.arange(0, DH, 2, dtype=np.float32) / np.float32(DH))
    angle = np.arange(N, dtype=np.float32)[:, None] * inv[None, :].astype(np.float32)
    cos, sin = (np.tile(np.repeat(f(angle), 2, 1).T, (2, 1)) for f in (np.cos, np.sin))
    sign = np.tile(np.array([-1.0, 1.0], np.float32), P // 2)[:, None]
    for name, table in (("cos", cos), ("sin", sin * sign)):
        arrays[f"rope_{name}_q"] = (table * np.float32(SCALE)).astype(np.float32)
        arrays[f"rope_{name}_k"] = table.astype(np.float32)
    arrays = {n: np.ascontiguousarray(v) for n, v in arrays.items()}

    nc = bacc.Bacc("TRN2", target_bir_lowering=False, num_devices=1)
    aps = {n: nc.dram_tensor(n + "_dram", v.shape, F32, kind="ExternalInput").ap()
           for n, v in arrays.items()}
    out = nc.dram_tensor("out_dram", (B, N, D), F32, kind="ExternalOutput").ap()
    build(nc, aps, out)
    r = run_bass_kernel_spmd(nc, [{n + "_dram": v for n, v in arrays.items()}], core_ids=[0])
    return r.results[0]["out_dram"]
```

```python
import concourse.bass as bass
import numpy as np
from concourse import mybir
from contextlib import ExitStack

F32 = mybir.dt.float32
F32R = mybir.dt.float32r
ALU = mybir.AluOpType
ACT = mybir.ActivationFunctionType
AX = mybir.AxisListType

B, N, D = 4, 512, 256
H, DH = 16, 64
J, DC = 64, 192
P = 128
TT = N // P
KT = D // P
HP = H // 2
CP = DC // 2
JT = N // P
TILES = 2 * TT
FT = 4 * D // P
LNS = 5
EPS = 1e-5
SCALE = DH ** -0.5

SUBLAYERS = ["self0", "cross0", "ff0", "self1", "cross1", "ff1"]
LN_OF = [0, 1, 2, 3, 3, 4]

PAIR = 2
JOBS = [(k, which) for k in range(6) for which in range(PAIR)]

SCORE_BANKS = [0, 1, 2, 3]
OUT_BANKS = [1, 2, 3, 2]
OUT_READ = {0: 0, 1: 1, 2: 4, 3: 3}
TRANSPOSE_BANKS = [4, 5]
O_BANK = 6
PROJ_BANK = 7


def build(nc, a, out):
    ctx = ExitStack()
    nc.disable_value_cache = True

    def sb(name, shape, dtype=F32):
        return ctx.enter_context(nc.sbuf_tensor(name, shape, dtype))

    def split(name, shape):
        return [sb(f"{name}_{part}", shape, F32R) for part in ("high", "low")]

    def sem(name):
        return ctx.enter_context(nc.semaphore(name))

    ident = sb("ident", [P, P])
    rope_cos, rope_sin = sb("rope_cos", [P, N]), sb("rope_sin", [P, N])
    cond_t = sb("cond_t", [P, KT, B])
    ada_w_or_probs_t = sb("ada_w_or_probs_t", [P, KT * 10 * D])
    ada_w = ada_w_or_probs_t[:, :].rearrange("p (t c) -> p t c", t=KT)
    probs_t = ada_w_or_probs_t[:, 0:2 * JT * N].rearrange("p (h j i) -> p h j i", h=2, j=JT)
    ada_vec = sb("ada_vec", [P, 28])
    ada_tmp = sb("ada_tmp", [P, 4, KT, B])
    coef = sb("coef", [P, B, LNS, 2, KT])
    coef_b = [sb(f"coef_b{i}", [P, LNS, 2, KT]) for i in range(PAIR)]
    out_bias = sb("out_bias", [P, 6, D])
    ff_bias = sb("ff_bias", [P, 3 * FT])
    ctx_stats, ctx_mv = sb("ctx_stats", [J, B, 6]), sb("ctx_mv", [J, B, 2])
    ctx_rstd = sb("ctx_rstd", [J, B, 1])
    ctx_vec = sb("ctx_vec", [CP, 2, 2])
    ctx_all = sb("ctx_all", [CP, 2, B, 2, J])
    ctx_b = [sb(f"ctx_b{i}", [CP, 2, 2, J]) for i in range(PAIR)]
    xs = [sb(f"x{i}", [P, TT, D]) for i in range(PAIR)]
    xn = sb("xn", [P, TT, D])
    stats, mv = sb("stats", [P, TT, 6]), sb("mv", [P, TT, 2])
    totals, apart = sb("totals", [P, TT, 2]), sb("apart", [P, TT, 1])
    rstd = sb("rstd", [P, TT, 1])
    half, eps = sb("half", [P, TT, 1]), sb("eps", [P, TT, 1])
    zero = sb("zero", [P, 1])
    h_t = sb("h_t", [P, KT, N])
    probs = sb("probs", [P, 4, N])
    ctx_rows = h_t[0:J, :, :].rearrange("p t n -> p (t n)")[:, 0:B * DC]\
        .rearrange("p (b d) -> p b d", b=B)
    ctx_norm = probs[0:J, 0:2, :].rearrange("p t n -> p (t n)")[:, 0:B * DC]\
        .rearrange("p (b d) -> p b d", b=B)
    hidden, hidden_gated = probs[:, 0:2, :], probs[:, 2:4, :]
    h_parts = [split(f"h{i}", [P, KT, N]) for i in range(PAIR)]
    inner_parts = split("inner", [P, HP, N])
    w_out = sb("w_out", [P, HP, D])
    w_out_parts = split("w_out", [P, HP, D])
    w_qkv = [sb(f"w_qkv{i}", [P, 3, KT, P]) for i in range(2)]
    w_qk_parts = [split(f"w_qk{i}", [P, 2, KT, P]) for i in range(2)]
    w_xq_parts = [split(f"w_xq{i}", [P, KT, P]) for i in range(2)]
    w_xq = [sb(f"w_xq{i}", [P, KT, P]) for i in range(2)]
    w_xkv = [sb(f"w_xkv{i}", [CP, 2, 2, P]) for i in range(2)]
    w_ff_or_rot = sb("w_ff_or_rot", [P, KT * 8 * D])
    w_ff = {2: w_ff_or_rot[:, :].rearrange("p (t c) -> p t c", t=KT),
            5: w_ff_or_rot[:, 0:KT * 4 * D].rearrange("p (t c) -> p t c", t=KT)}
    rot = w_ff_or_rot[:, KT * 4 * D:].rearrange("p (r n) -> p r n", r=4)
    q_t = [sb(f"q_t{i}", [P, N]) for i in range(2)]
    q_parts = [split(f"q{i}", [P, N]) for i in range(2)]
    k_parts = [split(f"k{i}", [P, N]) for i in range(2)]
    v_s = [sb(f"v_s{i}", [P, JT, P]) for i in range(2)]
    k_diag = [sb(f"k_diag{i}", [P, P]) for i in range(2)]
    v_diag = [sb(f"v_diag{i}", [P, P]) for i in range(2)]
    rot_k = sb("rot_k", [P, 2, J])
    neg_max, sums, recips = (sb(n, [P, TILES]) for n in ("neg_max", "sums", "recips"))

    bank = [ctx.enter_context(nc.psum_tensor(f"bank{i}", [P, 512], F32)) for i in range(8)]

    consts_in, tables_in = sem("consts_in"), sem("tables_in")
    setup_pool, setup_dve, setup_pe = sem("setup_pool"), sem("setup_dve"), sem("setup_pe")
    x_arrived = [sem(f"x_arrived{i}") for i in range(PAIR)]
    out_stored = sem("out_stored")
    w_out_in, w_out_split, w_ff_in = sem("w_out_in"), sem("w_out_split"), sem("w_ff_in")
    batch_ready = sem("batch_ready")
    row_stats = sem("row_stats")
    row_rstd = sem("row_rstd")
    normed = sem("normed")
    turned = sem("turned")
    biased = sem("biased")
    out_proj_done = sem("out_proj_done")
    x_updated = sem("x_updated")

    def nth(k, which, b):
        return b * 6 + (2 * k - 5 * which)

    class Signals:
        pass

    sig = []
    for k, name in enumerate(SUBLAYERS):
        s = Signals()
        s.h0 = sem(f"{name}_h0")
        s.h1 = sem(f"{name}_h1")
        if k in (2, 5):
            s.up = sem(f"{name}_up")
            s.gelu = sem(f"{name}_gelu")
            if k == 2:
                s.gated = sem(f"{name}_gated")
            s.high = sem(f"{name}_high")
            s.inner = sem(f"{name}_inner")
        else:
            s.w = [sem(f"{name}_w{i}") for i in range(2)]
            if k in (1, 4):
                s.w_kv = [sem(f"{name}_w_kv{i}") for i in range(2)]
            s.w_split = sem(f"{name}_w_split")
            s.q_proj = sem(f"{name}_q_proj")
            s.v_proj = sem(f"{name}_v_proj")
            s.q = sem(f"{name}_q")
            s.k = sem(f"{name}_k")
            s.v = sem(f"{name}_v")
            s.scores = sem(f"{name}_scores")
            s.neg_max = sem(f"{name}_neg_max")
            s.exp = sem(f"{name}_exp")
            s.recip = sem(f"{name}_recip")
            s.probs = sem(f"{name}_probs")
            s.probs_turned = sem(f"{name}_turned_p")
            s.probs_t = sem(f"{name}_probs_t")
            s.o = sem(f"{name}_o")
            s.inner = sem(f"{name}_inner")
            s.o_high = sem(f"{name}_o_high")
            if k in (0, 3):
                s.k_proj = sem(f"{name}_k_proj")
                s.q_high = sem(f"{name}_q_high")
                s.k_high = sem(f"{name}_k_high")
            else:
                s.shifted = sem(f"{name}_shifted")
                s.sums = sem(f"{name}_sums")
            if k >= 3:
                s.q_rot = sem(f"{name}_q_rot")
                s.k_rot = sem(f"{name}_k_rot")
                s.pool = sem(f"{name}_pool")
            if k == 3:
                s.q_sum = sem(f"{name}_q_sum")
                s.k_sum = sem(f"{name}_k_sum")
        sig.append(s)

    SWAP = [i ^ 1 for i in range(32)]
    block = ctx.enter_context(nc.Block())

    CONSTS = [(ident, "ident"), (cond_t, "cond_t"), (ada_w, "ada_w"), (ada_vec, "ada_vec"),
              (ctx_rows, "ctx_rows"), (ctx_vec, "ctx_vec")]
    TABLES = [(out_bias, "out_bias"), (ff_bias, "ff_bias"), (rope_cos, "rope_cos"),
              (rope_sin, "rope_sin")]

    def full(t):
        return t[tuple(slice(None) for _ in t.shape)]

    @block.sync
    def _(sp):
        def load_pair(k, slot, s):
            if k in (0, 3):
                sp.dma_start(w_qkv[slot][:, :, :, :], a[f"w_qkv{k // 3}"][s, :, :, :, :])\
                    .then_inc(sig[k].w[slot], 16)
            else:
                sp.dma_start(w_xq[slot][:, :, :], a[f"w_xq{k // 3}"][s, :, :, :])\
                    .then_inc(sig[k].w[slot], 16)

        def load_kv(k, slot, s):
            sp.dma_start(w_xkv[slot][:, :, :, :], a[f"w_xkv{k // 3}"][s, :, :, :, :])\
                .then_inc(sig[k].w_kv[slot], 16)

        def load_x(which, b):
            sp.dma_start(xs[which][:, :, :], a["x"][b, :, :].rearrange("(t p) d -> p t d", p=P))\
                .then_inc(x_arrived[which], 16)

        for which in range(PAIR):
            load_x(which, which)
        for dst, name in CONSTS:
            sp.dma_start(full(dst), a[name]).then_inc(consts_in, 16)
        sp.dma_start(ctx_all[:, 0, :, :, :], a["ctx_t"]).then_inc(consts_in, 16)

        for k in (0, 1):
            for s in range(2):
                load_pair(k, s, s)
                if k == 1:
                    load_kv(k, s, s)
            if k == 0:
                for dst, name in TABLES:
                    sp.dma_start(full(dst), a[name]).then_inc(tables_in, 16)

        def load_w_out(k):
            sp.dma_start(w_out[:, :, :], a[f"w_out{k}"]).then_inc(w_out_in, 16)

        load_w_out(0)
        sp.dma_start(w_ff[2][:, :, :], a["w_ff0"]).then_inc(w_ff_in, 16)
        for first_b in range(0, B, PAIR):
            for k, which in JOBS:
                b = first_b + which
                if k in (0, 1, 3, 4):
                    cross = k in (1, 4)
                    used, each = (sig[k].w_split, 2) if cross else (sig[k].v_proj, 1)
                    with sp.Fori(0, 3) as i:
                        for u in range(2):
                            sp.wait_ge(used, i * (2 * each) + (b * HP + u + 1) * each)
                            load_pair(k, u, i * 2 + (u + 2))
                            if cross:
                                sp.wait_ge(sig[k].v_proj, i * 2 + (b * HP + u + 1))
                                load_kv(k, u, i * 2 + (u + 2))
                    nxt = k if which == 0 else (k + 3) % 6
                    if not (k >= 3 and b == B - 1):
                        for u in range(2):
                            sp.wait_ge(used, (b * HP + HP - 1 + u) * each)
                            load_pair(nxt, u, u)
                            if cross:
                                sp.wait_ge(sig[k].v_proj, b * HP + HP - 1 + u)
                                load_kv(nxt, u, u)
                if which == 0 and not (k == 5 and b + PAIR > B - 1):
                    sp.wait_ge(w_out_split, (first_b // PAIR * 6 + k + 1) * 8)
                    load_w_out((k + 1) % 6)
                if (k, which) == (3, 0):
                    sp.wait_ge(sig[2].up, (first_b + PAIR) * FT)
                    sp.dma_start(w_ff[5], a["w_ff1"]).then_inc(w_ff_in, 16)
                if (k, which) == (0, 0) and first_b:
                    sp.wait_ge(sig[5].up, first_b * FT)
                    sp.dma_start(w_ff[2][:, :, :], a["w_ff0"]).then_inc(w_ff_in, 16)
                if k == 5:
                    sp.wait_ge(x_updated, nth(5, which, b) * TT + TT)
                    sp.dma_start(out[b, :, :].rearrange("(t p) d -> p t d", p=P),
                                 xs[which][:, :, :]).then_inc(out_stored, 16)
                    if b + PAIR < B:
                        sp.wait_ge(out_stored, 16 * (b + 1))
                        load_x(which, b + PAIR)
        sp.wait_ge(out_stored, 16 * B)

    @block.gpsimd
    def _(pool):
        pool.memset(half[:, :, :], -0.5).then_inc(setup_pool, 1)
        pool.memset(eps[:, :, :], EPS).then_inc(setup_pool, 1)
        pool.memset(zero[:, :], 0.0).then_inc(setup_pool, 1)
        for i, k in enumerate((1, 4)):
            pool.memset(rot_k[:, i, :], 0.0).then_inc(sig[k].inner, 1)
        for i in range(2):
            pool.memset(k_diag[i][:, :], 0.0).then_inc(setup_pool, 1)
            pool.memset(v_diag[i][:, :], 0.0).then_inc(setup_pool, 1)
        pool.wait_ge(setup_dve, 2 * B)
        pool.tensor_scalar(ctx_rstd[:, :, :], ctx_mv[:, :, 1:2], EPS, None, ALU.add)\
            .then_inc(setup_pool, 1)
        pool.wait_ge(setup_pool, 8)
        pool.tensor_tensor(ctx_rstd[:, :, :], ctx_rstd[:, :, :], half[0:J, :, :], ALU.pow)\
            .then_inc(setup_pool, 1)

        def norm_std(k, which, b):
            pool.wait_ge(row_stats, nth(k, which, b) * 8 + 8)
            pool.tensor_tensor(rstd[:, :, :], mv[:, :, 1:2], eps[:, :, :], ALU.add)\
                .then_inc(row_rstd, 1)
            pool.wait_ge(row_rstd, nth(k, which, b) * 2 + 1)
            pool.tensor_tensor(rstd[:, :, :], rstd[:, :, :], half[:, :, :], ALU.pow)\
                .then_inc(row_rstd, 1)

        def add_bias(k, which, b):
            x = xs[which]
            pool.wait_ge(normed, nth(k, which, b) * TT + TT)
            for t in range(TT):
                pool.tensor_tensor(x[:, t, :], x[:, t, :], out_bias[:, k, :], ALU.add)\
                    .then_inc(biased, 1)

        def round_to(high, raw):
            nothing = zero[:, 0:1]
            if len(raw.shape) == 3:
                nothing = nothing.unsqueeze(2)
            return pool.tensor_tensor(high, raw, nothing.to_broadcast(list(raw.shape)), ALU.add)

        def split_pair(k, g, par, second, fresh=False):
            s = sig[k]
            if not fresh:
                pool.wait_ge(s.k_proj if k in (0, 3) else s.q_proj, g - 1)
            if k in (0, 3):
                pool.wait_ge(s.w[par], g * 8 + (8 if second else 16))
                raw, *part = (t[:, 0:2, :, :].rearrange("p n t c -> p (n t c)")
                              for t in (w_qkv[par], *w_qk_parts[par]))
            else:
                pool.wait_ge(s.w[par], g * 8 + (8 if second else 16))
                raw, *part = (t[:, :, :].rearrange("p t c -> p (t c)")
                              for t in (w_xq[par], *w_xq_parts[par]))
            round_to(part[0], raw).then_inc(s.w_split, 1)
            pool.wait_ge(s.w_split, g * 2 + 1)
            pool.tensor_tensor(part[1], raw, part[0], ALU.subtract).then_inc(s.w_split, 1)

        def split_w_out(k, pp, c):
            pool.wait_ge(w_out_in, pp * 96 + (k + 1) * 16)
            if k:
                pool.wait_ge(out_proj_done, nth(k, 0, pp * PAIR) * TT)
            tiles = slice(c * 2, c * 2 + 2) if isinstance(c, int) else bass.ds(c * 2, 2)
            raw, *part = (t[:, tiles, :] for t in (w_out, *w_out_parts))
            round_to(part[0], raw).then_inc(w_out_split, 1)
            pool.wait_ge(w_out_split, pp * 48 + c * 2 + (8 * k + 1))
            pool.tensor_tensor(part[1], raw, part[0], ALU.subtract).then_inc(w_out_split, 1)

        def rotate(k, par, n, g):
            s = sig[k]
            pool.wait_ge(s.q_rot if n == 0 else s.k_rot, g * 2 + 2)
            at = 2 * (n if k == 3 else par)
            pool.tensor_tensor(rot[:, at + 1, :], rot[:, at + 1, :], rope_sin[:, :], ALU.mult)\
                .then_inc(s.pool, 1)
            pool.wait_ge(s.pool, g * 2 + (1 + n) if k == 3 else g + 1)
            dst = rot[:, 2 * n, :] if k == 3 else q_t[par][:, :]
            done = s.q if k == 4 else s.q_sum if n == 0 else s.k_sum
            pool.tensor_tensor(dst, rot[:, at, :], rot[:, at + 1, :], ALU.add).then_inc(done, 1)

        def rotate_pair(k, g, par):
            if k in (3, 4):
                rotate(k, par, 0, g)
            if k == 3:
                rotate(k, par, 1, g)

        def first_splits(nxt, which_pair):
            if nxt and nxt[0] % 3 != 2:
                k, which, b = nxt
                if not which_pair:
                    split_pair(k, b * HP, 0, False, which == 0)
                else:
                    split_pair(k, b * HP + 1, 1, True, which == 0)

        def self_attention(job, nxt, pp):
            k, which, b = job
            g = b * HP
            rotate_pair(k, g + 1, 1)
            split_pair(k, g + 2, 0, False)
            if nxt:
                norm_std(*nxt)
            rotate_pair(k, g + 2, 0)
            split_pair(k, g + 3, 1, True)
            with pool.Fori(0, 2) as i:
                for u in range(2):
                    rotate_pair(k, b * HP + i * 2 + (u + 3), 1 - u)
                    split_pair(k, b * HP + i * 2 + (u + 4), u, u == 1)
                    if which == 0:
                        split_w_out(k, pp, i * 2 + u)
            rotate_pair(k, g + 7, 1)
            first_splits(nxt, 0)
            first_splits(nxt, 1)
            if nxt:
                add_bias(*nxt)

        def cross_attention(job, nxt, pp):
            k, which, b = job
            g = b * HP
            split_pair(k, g + 2, 0, False)
            split_pair(k, g + 3, 1, True)
            rotate_pair(k, g + 2, 0)
            if nxt:
                norm_std(*nxt)
            with pool.Fori(0, 2) as i:
                for u in range(2):
                    split_pair(k, b * HP + i * 2 + (u + 4), u, u == 1)
                    rotate_pair(k, b * HP + i * 2 + (u + 3), 1 - u)
                    if which == 0:
                        split_w_out(k, pp, i * 2 + u)
            rotate_pair(k, g + 7, 1)
            first_splits(nxt, 0)
            first_splits(nxt, 1)
            if nxt:
                add_bias(*nxt)

        def feed_forward(job, nxt, pp):
            k, which, b = job
            if nxt:
                norm_std(*nxt)
            if which == 0:
                for c in range(4):
                    split_w_out(k, pp, c)
            first_splits(nxt, 0)
            first_splits(nxt, 1)
            if nxt:
                add_bias(*nxt)

        with pool.Fori(0, B // PAIR) as pp:
            jobs = [(k, which, pp * PAIR + which) for k, which in JOBS]
            norm_std(*jobs[0])
            first_splits(jobs[0], 0)
            first_splits(jobs[0], 1)
            add_bias(*jobs[0])
            for n, job in enumerate(jobs):
                k, _, b = job
                if k % 3 != 2:
                    rotate_pair(k, b * HP, 0)
                if k % 3 == 1:
                    rotate_pair(k, b * HP + 1, 1)
                (self_attention, cross_attention, feed_forward)[k % 3]\
                    (job, jobs[n + 1] if n + 1 < len(jobs) else None, pp)

    def over_pairs(eng, b, body, end):
        body(0, b * HP, 0, True, False)
        with eng.Fori(0, 3) as i:
            body(i * 2 + 1, b * HP + i * 2 + 1, 1, False, False)
            body(i * 2 + 2, b * HP + i * 2 + 2, 0, False, False)
        body(HP - 1, b * HP + (HP - 1), 1, False, True)
        end(b * HP + HP)

    def over_cross_pairs(eng, b, body, end):
        body(0, b * HP, 0, True, False, True)
        with eng.Fori(0, 2) as i:
            for u in range(2):
                body(i * 2 + (u + 1), b * HP + i * 2 + (u + 1), 1 - u, False, False, True)
        body(5, b * HP + 5, 1, False, False, True)
        body(6, b * HP + 6, 0, False, False, False)
        body(7, b * HP + 7, 1, False, True, False)
        end(b * HP + HP)

    def over_jobs(eng, begin, start, run, finish):
        with eng.Fori(0, B // PAIR) as pp:
            jobs = [(k, which, pp * PAIR + which) for k, which in JOBS]
            begin(*jobs[0])
            start(*jobs[0])
            for n, job in enumerate(jobs):
                nxt = jobs[n + 1] if n + 1 < len(jobs) else None
                run(job, nxt, jobs[n - 1] if n else None)
                if nxt:
                    start(*nxt)
                finish(*job)

    @block.tensor
    def _(pe):
        mm = pe.matmul
        PRODUCTS = ((0, 0), (0, 1), (1, 0))

        def mm_parts(to, terms):
            n = len(terms) * len(PRODUCTS)
            for i, (lhs, rhs) in enumerate(terms):
                for j, (x, y) in enumerate(PRODUCTS):
                    at = i * len(PRODUCTS) + j
                    ins = mm(to, lhs[x], rhs[y], start=(at == 0), stop=(at == n - 1))
            return ins

        def setup():
            pe.wait_ge(consts_in, 16 * (len(CONSTS) + 1))
            for m in range(10 * KT):
                for kt in range(KT):
                    ins = mm(bank[0][:, m * B:m * B + B], ada_w[:, kt, m * P:m * P + P],
                             cond_t[:, kt, :], start=(kt == 0), stop=(kt == KT - 1))
            ins.then_inc(setup_pe, 1)
            pe.wait_ge(setup_dve, 3 * B)
            for b in range(B):
                for c in range(2):
                    ins = pe.transpose(bank[1][0:CP, (b * 2 + c) * J:(b * 2 + c + 1) * J],
                                       ctx_norm[:, b, c * CP:c * CP + CP], ident[0:J, 0:J])
            ins.then_inc(setup_pe, 1)

        def norm_turn(k, which, b, c):
            for t in range(TT):
                if c == 0:
                    pe.wait_ge(normed, nth(k, which, b) * TT + (t + 1))
                ins = pe.transpose(bank[TRANSPOSE_BANKS[c]][:, t * P:t * P + P],
                                   xn[:, t, c * P:c * P + P], ident[:, :])
            ins.then_inc(turned, 1)

        def h_ready(k, b):
            if k % 3 == 2:
                pe.wait_ge(sig[k].h0, b + 1)
                pe.wait_ge(sig[k].h1, b + 1)
            else:
                pe.wait_ge(sig[k].h1, b * 4 + 4)

        def out_free(prev, banks):
            if prev:
                tiles = max(OUT_READ[i] for i in banks)
                if tiles:
                    pe.wait_ge(x_updated, nth(*prev) * TT + tiles)

        def out_proj(k, which, b):
            s = sig[k]
            pe.wait_ge(w_out_split, (b - which) * 24 + (8 * k + 8))
            pe.wait_ge(s.inner, b * HP + (HP if k % 3 != 1 else HP + 1))
            for t in range(TT):
                if t == 3:
                    pe.wait_ge(x_updated, nth(k, which, b) * TT + 2)
                tokens = slice(t * P, t * P + P)
                mm_parts(bank[OUT_BANKS[t]][:, 0:D],
                         [([x[:, kt, tokens] for x in inner_parts], [w[:, kt, :] for w in w_out_parts])
                          for kt in range(HP)]).then_inc(out_proj_done, 1)

        def project(s, par, n, h, to, done):
            mm_parts(bank[to][:, :], [([w[:, n, kt, :] for w in w_qk_parts[par]],
                                       [x[:, kt, :] for x in h]) for kt in range(KT)])\
                .then_inc(done, 1)

        def project_v(s, par, to=PROJ_BANK):
            for t in range(JT):
                for kt in range(KT):
                    ins = mm(bank[to][:, t * P:t * P + P], h_t[:, kt, t * P:t * P + P],
                             w_qkv[par][:, 2, kt, :], start=(kt == 0), stop=(kt == KT - 1))
            ins.then_inc(s.v_proj, 1)

        def self_start(k, which, b):
            s, h = sig[k], h_parts[which]
            h_ready(k, b)
            pe.wait_ge(s.w_split, b * (2 * HP) + 2)
            project(s, 0, 0, h, PROJ_BANK, s.q_proj)
            project(s, 0, 1, h, TRANSPOSE_BANKS[0], s.k_proj)
            project_v(s, 0, TRANSPOSE_BANKS[1])

        def self_attention(job, nxt, prev):
            k, which, b = job
            s, h = sig[k], h_parts[which]

            def read(done, rotated, g):
                if k == 3:
                    pe.wait_ge(rotated, g * 2 + 2)
                else:
                    pe.wait_ge(done, g + 1)

            def score(t, g, par, first):
                h, it = divmod(t, TT)
                if not (first and t < 4):
                    pe.wait_ge(s.exp, g * TILES + (t - 3))
                else:
                    out_free(prev, [SCORE_BANKS[t]])
                r = slice(DH * h, DH * h + DH)
                mm_parts(bank[SCORE_BANKS[t % 4]][:, :],
                         [([x[r, it * P:it * P + P] for x in q_parts[par]],
                           [x[r, :] for x in k_parts[par]])]).then_inc(s.scores, 1)

            def turn(t, g, first):
                pe.wait_ge(s.probs, g * TILES + (t + 1))
                if not (first and t < 2):
                    pe.wait_ge(s.probs_t, g * TILES + (t - 1))
                elif t == 1:
                    pe.wait_ge(s.v, g + 1)
                for jt in range(JT):
                    ins = pe.transpose(bank[TRANSPOSE_BANKS[t % 2]][:, jt * P:jt * P + P],
                                       probs[:, t % 4, jt * P:jt * P + P], ident[:, :])
                ins.then_inc(s.probs_turned, 1)

            def weigh(g, par):
                pe.wait_ge(s.probs_t, g * TILES)
                pe.wait_ge(s.v, g)
                for jt in range(JT):
                    for h in range(2):
                        ins = mm(bank[O_BANK][DH * h:DH * h + DH, :],
                                 v_s[par][:, jt, DH * h:DH * h + DH], probs_t[:, h, jt, :],
                                 start=(jt == 0), stop=(jt == JT - 1))
                ins.then_inc(s.o, 1)

            def body(sx, g, par, first, last):
                pe.wait_ge(s.q, g + 1)
                pe.wait_ge(s.k, g + 1)
                for t in range(4):
                    score(t, g, par, first)
                if not last:
                    pe.wait_ge(s.w_split, g * 2 + 4)
                    pe.wait_ge(s.v, g + 1)
                    project(s, 1 - par, 0, h, PROJ_BANK, s.q_proj)
                if not first:
                    weigh(g, 1 - par)
                for t in range(TILES):
                    turn(t, g, first)
                    if t == 1 and not last:
                        if not first:
                            pe.wait_ge(s.inner, g)
                        project(s, 1 - par, 1, h, O_BANK, s.k_proj)
                    if t + 4 < TILES:
                        score(t + 4, g, par, first)
                    if last:
                        continue
                    if t == 4:
                        read(s.q, s.q_rot if k == 3 else None, g + 1)
                        project_v(s, 1 - par)

            def end(g):
                if nxt:
                    for c in range(KT):
                        pe.wait_ge(s.probs_t, g * TILES - 1 + c)
                        norm_turn(*nxt, c)
                weigh(g, 1)

            over_pairs(pe, b, body, end)

        def front_q(k, which, g, par, to=PROJ_BANK, first=False):
            s, h = sig[k], h_parts[which]
            pe.wait_ge(s.w_split, g * 2 + 2)
            if not first:
                pe.wait_ge(s.q_rot if k == 4 else s.q, g * 2 if k == 4 else g)
            mm_parts(bank[to][:, :], [([w[:, kt, :] for w in w_xq_parts[par]],
                                       [x[:, kt, :] for x in h]) for kt in range(KT)])\
                .then_inc(s.q_proj, 1)

        def front_kv(k, which, g, par, second, first=False):
            s, c = sig[k], k // 3
            pe.wait_ge(s.w_kv[par], g * 8 + (8 if second else 16))
            if not first:
                pe.wait_ge(s.v, g)
                pe.wait_ge(s.k, g)
            for kt in range(2):
                mm(bank[0][:, 0:J], w_xkv[par][:, 0, kt, :], ctx_b[which][:, c, kt, :],
                   start=(kt == 0), stop=(kt == 1))
            for h in range(2):
                for kt in range(2):
                    ins = mm(bank[0][J * h:J * h + J, J + DH * h:J + DH * h + DH],
                             ctx_b[which][:, c, kt, :], w_xkv[par][:, 1, kt, DH * h:DH * h + DH],
                             start=(kt == 0), stop=(kt == 1))
            ins.then_inc(s.v_proj, 1)

        def cross_start(k, which, b):
            h_ready(k, b)
            front_q(k, which, b * HP, 0, first=True)
            front_kv(k, which, b * HP, 0, False, first=True)
            front_q(k, which, b * HP + 1, 1, TRANSPOSE_BANKS[0], first=True)

        def cross_attention(job, nxt, prev):
            k, which, b = job
            s = sig[k]

            def score(g, par):
                pe.wait_ge(s.q, g + 1)
                pe.wait_ge(s.k, g + 1)
                for it in range(TT):
                    ins = mm(bank[1 + par][:, it * P:it * P + P], q_t[par][:, it * P:it * P + P],
                             k_diag[par][:, :], start=True, stop=True)
                ins.then_inc(s.scores, 1)

            def turn(g, par):
                pe.wait_ge(s.probs, g + 1)
                for it in range(TT):
                    ins = pe.transpose(bank[TRANSPOSE_BANKS[par]][:, it * P:it * P + P],
                                       probs[:, 2 * par, it * P:it * P + P], ident[:, :])
                ins.then_inc(s.probs_turned, 1)

            def weigh(g, par):
                pe.wait_ge(s.probs_t, g + 1)
                pe.wait_ge(s.v, g + 1)
                pe.wait_ge(s.inner, g + 1)
                mm(bank[O_BANK][:, :], v_diag[par][:, :], probs_t[:, par, 0, :],
                   start=True, stop=True).then_inc(s.o, 1)

            def body(sx, g, par, first, last, ahead):
                if first:
                    out_free(prev, [1])
                score(g, par)
                if not first:
                    turn(g - 1, 1 - par)
                if first:
                    out_free(prev, [2])
                if not last:
                    front_kv(k, which, g + 1, 1 - par, not par)
                if ahead:
                    front_q(k, which, g + 2, par)
                if not first:
                    weigh(g - 1, 1 - par)

            def end(g):
                turn(g - 1, 1)
                if nxt:
                    norm_turn(*nxt, 0)
                    pe.wait_ge(s.probs_t, g)
                    norm_turn(*nxt, 1)
                weigh(g - 1, 1)

            over_cross_pairs(pe, b, body, end)

        def feed_forward(job, nxt, prev):
            k, which, b = job
            s = sig[k]
            free = s.gated if k == 2 else s.gelu
            pe.wait_ge(w_ff_in, (b - which) * 16 + (16 if k == 2 else 32))
            for m in range(FT):
                banks = [m % 2, 3 - m % 2]
                if m < 2:
                    out_free(prev, banks if k == 2 or m == 1 else banks[:1])
                else:
                    pe.wait_ge(free, b * FT + (m - 1))
                halves = (m, FT + m) if k == 2 else (m,)
                for to, col in zip(banks, halves):
                    for kt in range(KT):
                        ins = mm(bank[to][:, :], w_ff[k][:, kt, col * P:col * P + P],
                                 h_t[:, kt, :], start=(kt == 0), stop=(kt == KT - 1))
                ins.then_inc(s.up, 1)
            if nxt:
                for c in range(KT):
                    norm_turn(*nxt, c)

        def begin(k, which, b):
            for c in range(KT):
                norm_turn(k, which, b, c)

        setup()
        over_jobs(pe, begin,
                  lambda k, which, b: (self_start, cross_start, lambda *_: h_ready(k, b))[k % 3]
                  (k, which, b),
                  lambda job, nxt, prev: (self_attention, cross_attention, feed_forward)[job[0] % 3]
                  (job, nxt, prev), out_proj)

    @block.scalar
    def _(act):
        def h_out(k, which, b):
            s = sig[k]
            act.wait_ge(turned, nth(k, which, b) * KT + 1)
            act.activation(h_t[:, 0, :], bank[TRANSPOSE_BANKS[0]][:, :], ACT.Identity,
                           bias=coef_b[which][:, LN_OF[k], 1, 0:1],
                           scale=coef_b[which][:, LN_OF[k], 0, 0:1]).then_inc(s.h0, 1)
            if k % 3 != 2:
                act.wait_ge(s.h0, b * 2 + 1)
                act.activation(h_parts[which][0][:, 0, :], h_t[:, 0, :], ACT.Copy).then_inc(s.h0, 1)

        def q_high(k, g, par, n, src):
            s = sig[k]
            if k == 3:
                act.wait_ge(s.q_sum if n == 0 else s.k_sum, g + 1)
                src = rot[:, 2 * n, :]
            else:
                act.wait_ge(s.q_proj if n == 0 else s.k_proj, g + 1)
                src = bank[src][:, :]
            act.activation((q_parts, k_parts)[n][par][0][:, :], src, ACT.Copy,
                           scale=SCALE if n == 0 else 1.0)\
                .then_inc(s.q_high if n == 0 else s.k_high, 1)

        def v_out(k, g, par, src=PROJ_BANK):
            act.wait_ge(sig[k].v_proj, g + 1)
            act.activation(v_s[par][:, :, :], bank[src][:, :], ACT.Copy).then_inc(sig[k].v, 1)

        def self_start(k, which, b):
            q_high(k, b * HP, 0, 0, PROJ_BANK)
            q_high(k, b * HP, 0, 1, TRANSPOSE_BANKS[0])
            v_out(k, b * HP, 0, TRANSPOSE_BANKS[1])

        def self_attention(job, nxt):
            k, which, b = job
            s = sig[k]

            def exp(t, g):
                act.wait_ge(s.neg_max, g * TILES + (t + 1))
                act.activation(probs[:, t % 4, :], bank[SCORE_BANKS[t % 4]][:, :], ACT.Exp,
                               bias=neg_max[:, t:t + 1], scale=1.0, accum_out=sums[:, t:t + 1])\
                    .then_inc(s.exp, 1)

            def turned_out(t, g):
                h, it = divmod(t, TT)
                act.wait_ge(s.probs_turned, g * TILES + (t + 1))
                act.activation(probs_t[:, h, :, it * P:it * P + P],
                               bank[TRANSPOSE_BANKS[t % 2]][:, :].rearrange("p (j i) -> p j i", j=JT),
                               ACT.Copy).then_inc(s.probs_t, 1)

            def o_high(sx, g):
                act.wait_ge(s.o, g)
                act.activation(inner_parts[0][:, sx, :], bank[O_BANK][:, :], ACT.Copy)\
                    .then_inc(s.o_high, 1)

            def body(sx, g, par, first, last):
                for t in range(4):
                    exp(t, g)
                if k == 0 and not last:
                    q_high(k, g + 1, 1 - par, 0, PROJ_BANK)
                if not first:
                    o_high(sx - 1, g)
                for t in range(TILES):
                    turned_out(t, g)
                    if t == 0:
                        exp(4, g)
                    if not last:
                        if k == 3 and t == 1:
                            q_high(k, g + 1, 1 - par, 0, PROJ_BANK)
                        if t == (1 if k == 0 else 4):
                            q_high(k, g + 1, 1 - par, 1, O_BANK)
                        if t == 6:
                            v_out(k, g + 1, 1 - par)
                    if 2 <= t <= 4:
                        exp(t + 3, g)

            def end(g):
                if nxt:
                    h_out(*nxt)
                o_high(HP - 1, g)

            over_pairs(act, b, body, end)

        def q_out(k, g, par, src=PROJ_BANK):
            if k == 1:
                act.wait_ge(sig[k].q_proj, g + 1)
                act.activation(q_t[par][:, :], bank[src][:, :], ACT.Copy).then_inc(sig[k].q, 1)

        def ctx_v_out(k, g, par):
            act.wait_ge(sig[k].v_proj, g + 1)
            act.wait_ge(sig[k].k, g + 1)
            for h in range(2):
                r = slice(J * h, J * h + J)
                ins = act.activation(v_diag[par][r, DH * h:DH * h + DH],
                                     bank[0][r, J + DH * h:J + DH * h + DH], ACT.Copy)
            ins.then_inc(sig[k].v, 1)

        def cross_start(k, which, b):
            q_out(k, b * HP, 0)
            ctx_v_out(k, b * HP, 0)
            q_out(k, b * HP + 1, 1, TRANSPOSE_BANKS[0])

        def cross_attention(job, nxt):
            k, which, b = job
            s = sig[k]

            def turned_out(g, par):
                act.wait_ge(s.probs_turned, g + 1)
                act.activation(probs_t[:, par, 0, :], bank[TRANSPOSE_BANKS[par]][:, :], ACT.Copy)\
                    .then_inc(s.probs_t, 1)

            def o_high(sx, g):
                act.wait_ge(s.o, g)
                act.activation(inner_parts[0][:, sx, :], bank[O_BANK][:, :], ACT.Copy)\
                    .then_inc(s.o_high, 1)

            def body(sx, g, par, first, last, ahead):
                if not first:
                    turned_out(g - 1, 1 - par)
                act.wait_ge(s.shifted, g + 1)
                act.activation(probs[:, 2 * par, :], probs[:, 2 * par + 1, :], ACT.Exp, scale=SCALE)\
                    .then_inc(s.exp, 1)
                if ahead:
                    q_out(k, g + 2, par)
                if not first:
                    o_high(sx - 1, g)
                if not last:
                    ctx_v_out(k, g + 1, 1 - par)

            def end(g):
                turned_out(g - 1, 1)
                if nxt:
                    h_out(*nxt)
                o_high(HP - 1, g)

            over_cross_pairs(act, b, body, end)

        def feed_forward(job, nxt):
            k, which, b = job
            s = sig[k]
            for m in range(FT):
                act.wait_ge(s.up, b * FT + (m + 1))
                if k == 2:
                    if m >= 2:
                        act.wait_ge(s.gated, b * FT + (m - 1))
                    src, bias = bank[3 - m % 2], ff_bias[:, FT + m:FT + m + 1]
                else:
                    if m >= 2:
                        act.wait_ge(s.inner, b * FT + (m - 1))
                    src, bias = bank[m % 2], ff_bias[:, 2 * FT + m:2 * FT + m + 1]
                dst = hidden[:, m % 2, :]
                act.activation(dst, src[:, :], ACT.Gelu, bias=bias, scale=1.0).then_inc(s.gelu, 1)
            if nxt:
                h_out(*nxt)

        def begin(k, which, b):
            act.wait_ge(batch_ready, b * 2 + 4)
            h_out(k, which, b)

        over_jobs(act, begin,
                  lambda k, which, b: (self_start, cross_start, lambda *_: None)[k % 3](k, which, b),
                  lambda job, nxt, prev: (self_attention, cross_attention, feed_forward)[job[0] % 3]
                  (job, nxt), lambda *_: None)

    @block.vector
    def _(dve):
        def setup():
            dve.wait_ge(consts_in, 16 * (len(CONSTS) + 1))
            for b in range(B):
                dve.bn_stats(ctx_stats[:, b, :], ctx_rows[:, b, :]).then_inc(setup_dve, 1)
            dve.wait_ge(setup_dve, B)
            for b in range(B):
                dve.bn_aggr(ctx_mv[:, b, :], ctx_stats[:, b, :]).then_inc(setup_dve, 1)
            dve.wait_ge(setup_dve, 2 * B)
            dve.wait_ge(setup_pool, 9)
            for b in range(B):
                dve.tensor_scalar(ctx_norm[:, b, :], ctx_rows[:, b, :], ctx_mv[:, b, 0:1],
                                  ctx_rstd[:, b, :], ALU.subtract, ALU.mult).then_inc(setup_dve, 1)
            dve.wait_ge(setup_pe, 1)
            emb = bank[0][:, 0:10 * KT * B].rearrange("p (m b) -> p m b", b=B)
            for n in range(3):
                for c in range(KT):
                    v = 4 * n + c
                    dve.tensor_scalar(coef[:, :, n, 0, c], emb[:, v, :], ada_vec[:, v:v + 1], 1.0,
                                      ALU.add, ALU.add)
                    ins = dve.tensor_scalar(coef[:, :, n, 1, c], emb[:, v + 2, :],
                                            ada_vec[:, v + 2:v + 3], None, ALU.add)
            for n in range(2):
                for c in range(KT):
                    m = 12 + 4 * n + c
                    dve.tensor_scalar(ada_tmp[:, 2 * n, c, :], emb[:, m, :], vec(n, c, 0), 1.0,
                                      ALU.add, ALU.add).then_inc(setup_dve, 1)
                    dve.tensor_scalar(ada_tmp[:, 2 * n + 1, c, :], emb[:, m + 2, :], vec(n, c, 1),
                                      None, ALU.add).then_inc(setup_dve, 1)
            dve.wait_ge(setup_dve, 3 * B + 8)
            for n in range(2):
                for c in range(KT):
                    dve.tensor_scalar(coef[:, :, 3 + n, 0, c], ada_tmp[:, 2 * n, c, :], vec(n, c, 2),
                                      None, ALU.mult).then_inc(setup_dve, 1)
                    dve.scalar_tensor_tensor(out=coef[:, :, 3 + n, 1, c],
                                             in0=ada_tmp[:, 2 * n, c, :], scalar=vec(n, c, 3),
                                             in1=ada_tmp[:, 2 * n + 1, c, :], op0=ALU.mult,
                                             op1=ALU.add).then_inc(setup_dve, 1)
            dve.wait_ge(setup_pe, 2)
            turned = bank[1][0:CP, :].rearrange("p (b c j) -> p b c j", b=B, c=2)
            for c in range(2):
                dve.tensor_scalar(ctx_all[:, 1, :, c, :], turned[:, :, c, :], ctx_vec[:, 0, c:c + 1],
                                  ctx_vec[:, 1, c:c + 1], ALU.mult, ALU.add).then_inc(setup_dve, 1)
            dve.wait_ge(setup_dve, 3 * B + 18)
            dve.wait_ge(tables_in, 16 * len(TABLES))

        def vec(n, c, i):
            at = 12 + (n * 4 + i) * KT + c
            return ada_vec[:, at:at + 1]

        def norm_stats(k, which, b):
            s, x = sig[k], xs[which]
            if k == 0:
                dve.wait_ge(x_arrived[which], (b + (2 - which)) * 8)
            else:
                dve.wait_ge(x_updated, nth(k - 1, which, b) * TT + TT)
            for t in range(TT):
                dve.bn_stats(stats[:, t, :], x[:, t, :]).then_inc(row_stats, 1)
            dve.wait_ge(row_stats, nth(k, which, b) * 8 + 4)
            dve.tensor_tensor(totals[:, :, :], stats[:, :, 1:3], stats[:, :, 4:6], ALU.add)\
                .then_inc(row_stats, 1)
            dve.tensor_tensor(apart[:, :, :], stats[:, :, 1:2], stats[:, :, 4:5], ALU.subtract)\
                .then_inc(row_stats, 1)
            dve.wait_ge(row_stats, nth(k, which, b) * 8 + 6)
            dve.tensor_scalar(mv[:, :, 0:1], totals[:, :, 0:1], 0.5, None, ALU.mult)
            dve.scalar_tensor_tensor(out=apart[:, :, :], in0=apart[:, :, :], scalar=0.25,
                                     in1=apart[:, :, :], op0=ALU.mult, op1=ALU.mult)\
                .then_inc(row_stats, 1)
            dve.wait_ge(row_stats, nth(k, which, b) * 8 + 7)
            dve.scalar_tensor_tensor(out=mv[:, :, 1:2], in0=totals[:, :, 1:2], scalar=1.0 / D,
                                     in1=apart[:, :, :], op0=ALU.mult, op1=ALU.add)\
                .then_inc(row_stats, 1)

        def norm_apply(k, which, b):
            s, x = sig[k], xs[which]
            dve.wait_ge(row_rstd, nth(k, which, b) * 2 + 2)
            for t in range(TT):
                dve.tensor_scalar(xn[:, t, :], x[:, t, :], mv[:, t, 0:1], rstd[:, t, :],
                                  ALU.subtract, ALU.mult).then_inc(normed, 1)

        def h_out(k, which, b):
            s = sig[k]
            dve.wait_ge(turned, nth(k, which, b) * KT + 2)
            dve.tensor_scalar(h_t[:, 1, :], bank[TRANSPOSE_BANKS[1]][:, :],
                              coef_b[which][:, LN_OF[k], 0, 1:2],
                              coef_b[which][:, LN_OF[k], 1, 1:2], ALU.mult, ALU.add)\
                .then_inc(s.h1, 1)
            if k % 3 != 2:
                high, low = h_parts[which]
                dve.wait_ge(s.h1, b * 4 + 1)
                dve.tensor_copy(high[:, 1, :], h_t[:, 1, :]).then_inc(s.h1, 1)
                dve.wait_ge(s.h1, b * 4 + 2)
                dve.tensor_tensor(low[:, 1, :], h_t[:, 1, :], high[:, 1, :], ALU.subtract)\
                    .then_inc(s.h1, 1)
                dve.wait_ge(s.h0, b * 2 + 2)
                dve.tensor_tensor(low[:, 0, :], h_t[:, 0, :], high[:, 0, :], ALU.subtract)\
                    .then_inc(s.h1, 1)

        def residual(k, which, b):
            s, x = sig[k], xs[which]
            dve.wait_ge(biased, nth(k, which, b) * TT + TT)
            for t in range(TT):
                dve.wait_ge(out_proj_done, nth(k, which, b) * TT + (t + 1))
                dve.tensor_tensor(x[:, t, :], bank[OUT_BANKS[t]][:, 0:D], x[:, t, :], ALU.add)\
                    .then_inc(x_updated, 1)

        def o_low(s, sx, g):
            dve.wait_ge(s.o_high, g)
            dve.tensor_tensor(inner_parts[1][:, sx, :], bank[O_BANK][:, :],
                              inner_parts[0][:, sx, :], ALU.subtract).then_inc(s.inner, 1)

        def rope(k, n, g, src=PROJ_BANK):
            s = sig[k]
            parts = s.q_rot if n == 0 else s.k_rot
            dve.wait_ge(s.q_proj if n == 0 else s.k_proj, g + 1)
            dve.tensor_tensor(rot[:, 2 * n, :], bank[src][:, :], rope_cos[:, :], ALU.mult)\
                .then_inc(parts, 1)
            dve.stream_shuffle(rot[:, 2 * n + 1, :], bank[src][:, :], SWAP).then_inc(parts, 1)

        def q_low(k, g, par, n, src=PROJ_BANK):
            s = sig[k]
            high, low = (q_parts, k_parts)[n][par]
            dve.wait_ge(s.q_high if n == 0 else s.k_high, g + 1)
            whole = rot[:, 2 * n, :] if k == 3 else bank[src][:, :]
            done = s.q if n == 0 else s.k
            if n == 0:
                dve.scalar_tensor_tensor(out=low[:, :], in0=whole, scalar=SCALE, in1=high[:, :],
                                         op0=ALU.mult, op1=ALU.subtract).then_inc(done, 1)
            else:
                dve.tensor_tensor(low[:, :], whole, high[:, :], ALU.subtract).then_inc(done, 1)

        def self_start(k, which, b):
            for n, src in ((0, PROJ_BANK), (1, TRANSPOSE_BANKS[0])):
                if k == 3:
                    rope(k, n, b * HP, src)
                else:
                    q_low(k, b * HP, 0, n, src)
            if k == 3:
                q_low(k, b * HP, 0, 0)
                q_low(k, b * HP, 0, 1)

        def self_attention(job, nxt):
            k, which, b = job
            s = sig[k]

            def row_max(t, g):
                dve.wait_ge(s.scores, g * TILES + (t + 1))
                dve.tensor_reduce(neg_max[:, t:t + 1], bank[SCORE_BANKS[t % 4]][:, :], AX.X,
                                  ALU.max, negate=True).then_inc(s.neg_max, 1)

            def normalise(t, g):
                dve.wait_ge(s.exp, g * TILES + (t + 1))
                dve.reciprocal(recips[:, t:t + 1], sums[:, t:t + 1]).then_inc(s.recip, 1)
                dve.wait_ge(s.recip, g * TILES + (t + 1))
                dve.tensor_scalar(probs[:, t % 4, :], probs[:, t % 4, :], recips[:, t:t + 1], None,
                                  ALU.mult).then_inc(s.probs, 1)

            def body(sx, g, par, first, last):
                for t in range(3):
                    row_max(t, g)
                normalise(0, g)
                row_max(3, g)
                normalise(1, g)
                if k == 3 and not last:
                    rope(k, 0, g + 1)
                normalise(2, g)
                normalise(3, g)
                if k == 0 and not last:
                    q_low(k, g + 1, 1 - par, 0)
                if last and nxt:
                    norm_apply(*nxt)
                if not first:
                    o_low(s, sx - 1, g)
                row_max(4, g)
                if first and nxt:
                    norm_stats(*nxt)
                if k == 3 and not last:
                    rope(k, 1, g + 1, O_BANK)
                row_max(5, g)
                normalise(4, g)
                if k == 0 and not last:
                    q_low(k, g + 1, 1 - par, 1, O_BANK)
                row_max(6, g)
                normalise(5, g)
                row_max(7, g)
                if k == 3 and not last:
                    q_low(k, g + 1, 1 - par, 0)
                normalise(6, g)
                normalise(7, g)
                if k == 3 and not last:
                    q_low(k, g + 1, 1 - par, 1)

            def end(g):
                if nxt:
                    h_out(*nxt)
                o_low(s, HP - 1, g)

            over_pairs(dve, b, body, end)

        def cross_q_out(k, g, par, src=PROJ_BANK):
            if k == 4:
                s = sig[k]
                dve.wait_ge(s.q_proj, g + 1)
                dve.tensor_tensor(rot[:, 2 * par, :], bank[src][:, :], rope_cos[:, :],
                                  ALU.mult).then_inc(s.q_rot, 1)
                dve.stream_shuffle(rot[:, 2 * par + 1, :], bank[src][:, :], SWAP)\
                    .then_inc(s.q_rot, 1)

        def ctx_k_out(k, g, par):
            s = sig[k]
            dve.wait_ge(s.v_proj, g + 1)
            src = bank[0][:, 0:J]
            if k == 4:
                dve.tensor_tensor(rot_k[:, 0, :], src, rope_cos[:, 0:J], ALU.mult)\
                    .then_inc(s.k_rot, 1)
                dve.stream_shuffle(rot_k[:, 1, :], src, SWAP).then_inc(s.k_rot, 1)
                dve.wait_ge(s.k_rot, g * 3 + 2)
                dve.tensor_tensor(rot_k[:, 1, :], rot_k[:, 1, :], rope_sin[:, 0:J], ALU.mult)\
                    .then_inc(s.k_rot, 1)
                dve.wait_ge(s.k_rot, g * 3 + 3)
            for h in range(2):
                r = slice(DH * h, DH * h + DH)
                c = slice(J * h, J * h + J)
                if k == 4:
                    ins = dve.tensor_tensor(k_diag[par][r, c], rot_k[r, 0, :], rot_k[r, 1, :],
                                            ALU.add)
                else:
                    ins = dve.tensor_copy(k_diag[par][r, c], bank[0][r, 0:J])
            ins.then_inc(s.k, 1)

        def cross_start(k, which, b):
            cross_q_out(k, b * HP, 0)
            ctx_k_out(k, b * HP, 0)
            cross_q_out(k, b * HP + 1, 1, TRANSPOSE_BANKS[0])

        def cross_attention(job, nxt):
            k, which, b = job
            s = sig[k]
            rows = 2 * TT

            def by_row(ap):
                return ap.rearrange("p (r j) -> p r j", j=J)

            def across(ap):
                return ap.unsqueeze(2).to_broadcast([P, rows, J])

            def softmax_a(g, par):
                dve.wait_ge(s.scores, g + 1)
                dve.tensor_reduce(neg_max[:, :], by_row(bank[1 + par][:, :]), AX.X, ALU.max,
                                  negate=True).then_inc(s.neg_max, 1)
                dve.wait_ge(s.neg_max, g + 1)
                dve.tensor_tensor(by_row(probs[:, 2 * par + 1, :]), by_row(bank[1 + par][:, :]),
                                  across(neg_max[:, :]), ALU.add).then_inc(s.shifted, 1)

            def softmax_b(g, par):
                dve.wait_ge(s.exp, g + 1)
                dve.tensor_reduce(sums[:, :], by_row(probs[:, 2 * par, :]), AX.X, ALU.add)\
                    .then_inc(s.sums, 1)
                dve.wait_ge(s.sums, g + 1)
                dve.reciprocal(recips[:, :], sums[:, :]).then_inc(s.recip, 1)
                dve.wait_ge(s.recip, g + 1)
                dve.tensor_tensor(by_row(probs[:, 2 * par, :]), by_row(probs[:, 2 * par, :]),
                                  across(recips[:, :]), ALU.mult).then_inc(s.probs, 1)

            def body(sx, g, par, first, last, ahead):
                softmax_a(g, par)
                if last and nxt:
                    norm_apply(*nxt)
                if not last:
                    ctx_k_out(k, g + 1, 1 - par)
                if ahead:
                    cross_q_out(k, g + 2, par)
                softmax_b(g, par)
                if first and nxt:
                    norm_stats(*nxt)
                if not first:
                    o_low(s, sx - 1, g)

            def end(g):
                if nxt:
                    h_out(*nxt)
                o_low(s, HP - 1, g)

            over_cross_pairs(dve, b, body, end)

        def feed_forward(job, nxt):
            k, which, b = job
            s = sig[k]
            if nxt:
                norm_stats(*nxt)
            for m in range(FT):
                tmp = hidden[:, m % 2, :]
                dve.wait_ge(s.gelu, b * FT + (m + 1))
                if k == 2:
                    tmp = hidden_gated[:, m % 2, :]
                    dve.scalar_tensor_tensor(out=tmp, in0=bank[m % 2][:, :],
                                             scalar=ff_bias[:, m:m + 1], in1=hidden[:, m % 2, :],
                                             op0=ALU.add, op1=ALU.mult).then_inc(s.gated, 1)
                    dve.wait_ge(s.gated, b * FT + (m + 1))
                high, low = (t[:, m, :] for t in inner_parts)
                dve.tensor_copy(high, tmp).then_inc(s.high, 1)
                dve.wait_ge(s.high, b * FT + (m + 1))
                dve.tensor_tensor(low, tmp, high, ALU.subtract).then_inc(s.inner, 1)
                if m == 3 and nxt:
                    norm_apply(*nxt)
            if nxt:
                h_out(*nxt)

        setup()

        def begin(k, which, b):
            for i in range(PAIR):
                dve.tensor_copy(coef_b[i][:, :, :, :], coef[:, b + i, :, :, :])\
                    .then_inc(batch_ready, 1)
                dve.tensor_copy(ctx_b[i][:, :, :, :], ctx_all[:, :, b + i, :, :])\
                    .then_inc(batch_ready, 1)
            dve.wait_ge(batch_ready, b * 2 + 4)
            norm_stats(k, which, b)
            norm_apply(k, which, b)
            h_out(k, which, b)

        over_jobs(dve, begin,
                  lambda k, which, b: (self_start, cross_start, lambda *_: None)[k % 3](k, which, b),
                  lambda job, nxt, prev: (self_attention, cross_attention, feed_forward)[job[0] % 3]
                  (job, nxt), residual)

    ctx.close()


def kernel(**inputs):
    import concourse.bacc as bacc
    from concourse.bass_utils import run_bass_kernel_spmd

    g = {n: np.asarray(v) for n, v in inputs.items()}
    l0 = {n[9:]: v for n, v in g.items() if n.startswith("L0_xcond_")}
    l1 = {n[9:]: v for n, v in g.items() if n.startswith("L1_xcond_")}

    def by_partition(w, p=P):
        return w.reshape(-1, p, w.shape[1]).transpose(1, 0, 2)

    def columns(v, p=P):
        return v.reshape(-1, p).T

    def per_pair(w, p=P):
        t = w.shape[0] // p
        return w.reshape(t, p, HP, P).transpose(2, 1, 0, 3)

    inner = H * DH
    arrays = {
        "x": g["x"],
        "cond_t": by_partition(g["cond_1024"].T),
        "ctx_rows": g["ctx_768"].transpose(1, 0, 2),
        "ctx_t": g["ctx_768"].reshape(B, J, 2, CP).transpose(3, 0, 2, 1),
        "ident": np.eye(P, dtype=np.float32),
        "ada_w": by_partition(np.concatenate(
            [l0["n1_w"], l0["n2_w"], l0["n3_w"], l1["g1_w"], l1["b1_w"], l1["g2_w"], l1["b2_w"]], 1)),
        "ada_vec": np.concatenate([columns(v) for v in (
            l0["n1_b"], l0["n2_b"], l0["n3_b"], l1["g1_b"], l1["b1_b"], l1["ln1_w"], l1["ln1_b"],
            l1["g2_b"], l1["b2_b"], l1["ln2_w"], l1["ln2_b"])], 1),
        "ctx_vec": np.stack([columns(l1["ca_lnc_w"], CP), columns(l1["ca_lnc_b"], CP)], 1),
        "out_bias": np.broadcast_to(np.stack(
            [l0["o1_b"], l0["o2_b"], l0["ff_b2"], l1["sa_bo"], l1["ca_bo"], l1["ff_b2"]]), (P, 6, D)),
        "ff_bias": np.concatenate([columns(l0["ff_b1"]), columns(l1["ff_b1"])], 1),
        "w_ff0": by_partition(l0["ff_w1"]),
        "w_ff1": by_partition(l1["ff_w1"]),
    }
    for k, w in enumerate((l0["o1_w"], l0["o2_w"], l0["ff_w2"], l1["sa_wo"], l1["ca_wo"],
                           l1["ff_w2"])):
        arrays[f"w_out{k}"] = by_partition(w)
    qkv = [(l0["q1"], l0["k1"], l0["v1"]),
           (l1["sa_wq"], l1["sa_wkv"][:, :inner], l1["sa_wkv"][:, inner:])]
    cross = [(l0["q2"], l0["k2"], l0["v2"]),
             (l1["ca_wq"], l1["ca_wkv"][:, :inner], l1["ca_wkv"][:, inner:])]
    for n in range(2):
        arrays[f"w_qkv{n}"] = np.stack([per_pair(w) for w in qkv[n]], 2)
        arrays[f"w_xq{n}"] = per_pair(cross[n][0])
        arrays[f"w_xkv{n}"] = np.stack([per_pair(w, CP) for w in cross[n][1:]], 2)

    inv = np.float32(1.0) / np.power(np.float32(10000.0),
                                     np.arange(0, DH, 2, dtype=np.float32) / np.float32(DH))
    angle = np.arange(N, dtype=np.float32)[:, None] * inv[None, :].astype(np.float32)
    cos, sin = (np.tile(np.repeat(f(angle), 2, 1).T, (2, 1)) for f in (np.cos, np.sin))
    sign = np.tile(np.array([-1.0, 1.0], np.float32), P // 2)[:, None]
    arrays["rope_cos"], arrays["rope_sin"] = cos, (sin * sign).astype(np.float32)
    arrays = {n: np.ascontiguousarray(v) for n, v in arrays.items()}

    nc = bacc.Bacc("TRN2", target_bir_lowering=False, num_devices=1)
    aps = {n: nc.dram_tensor(n + "_dram", v.shape, F32, kind="ExternalInput").ap()
           for n, v in arrays.items()}
    out = nc.dram_tensor("out_dram", (B, N, D), F32, kind="ExternalOutput").ap()
    build(nc, aps, out)
    r = run_bass_kernel_spmd(nc, [{n + "_dram": v for n, v in arrays.items()}], core_ids=[0])
    return r.results[0]["out_dram"]
```
